# Optimizing a Trainium2 kernel written in Bass

```python
import numpy as np
import jax
import jax.numpy as jnp

def _softmax(x, axis=-1):
    return jax.nn.softmax(x, axis=axis)
def _gelu(x):
    return jax.nn.gelu(x, approximate=True)
def _silu(x):
    return jax.nn.silu(x)
def _sigmoid(x):
    return jax.nn.sigmoid(x)
def _layernorm(x, axis=-1, eps=1e-5):
    m = jnp.mean(x, axis=axis, keepdims=True)
    v = jnp.var(x, axis=axis, keepdims=True)
    return (x - m) / jnp.sqrt(v + eps)
def _scatter_add(tgt, idx, src, axis=0):
    return tgt.at[idx].add(src)
def _segment_sum(src, seg, n):
    return jax.ops.segment_sum(src, seg, n)

kernel_name = 'mk_adj_resnorm_d4_adj_128_d11013'

def setup_inputs(seed: int = 0):
    np.random.seed(seed)
    _w = jnp.asarray
    def _rec_inputs():
        import jax
        import jax.numpy as jnp
        _gk = jax.random.key(seed)
        x = -0.000929 + 1 * jax.random.normal(jax.random.fold_in(_gk, 1), (8192, 128), jnp.float32)
        _a = jax.random.bernoulli(jax.random.fold_in(_gk, 2), 0.00195312, (8192, 8192))
        _a = jnp.logical_or(_a, jnp.swapaxes(_a, -1, -2))
        _a = jnp.logical_or(_a, jnp.eye(8192, dtype=bool))
        adj = _a.astype(jnp.int32)
        return x, adj
    x, adj = _rec_inputs()
    def _L0_gnn_setup():
        import jax
        import jax.numpy as jnp
        import numpy as np
        from jax import lax
        N = 8192
        F = 128
        CHUNK = 64
        key = jax.random.key(seed)
        kx, ka = jax.random.split(key)
        X = jax.random.normal(kx, (N, F), dtype=jnp.float32)
        adj = jax.random.randint(ka, (N, N), 0, 2, dtype=jnp.int32)
        return {'X': X, 'adj': adj}
    _L0_gnn_all = _L0_gnn_setup()
    _L0_gnn_in = {k: v for k, v in _L0_gnn_all.items() if k in ()}
    del _L0_gnn_all

    def _L1_gnn_setup():
        import jax, jax.numpy as jnp
        import numpy as np
        N = 8192
        IN = 128
        OUT = 128
        THR = 0.0001
        ALPHA = 0.2
        NEG = -1000000000.0
        key = jax.random.key(seed)
        k1, k2, k3, k4 = jax.random.split(key, 4)
        inp = jax.random.normal(k1, (N, IN), jnp.float32)
        W = jax.random.normal(k2, (IN, OUT), jnp.float32) * (1.414 * np.sqrt(2.0 / (IN + OUT)))
        a = jax.random.normal(k3, (2 * OUT, 1), jnp.float32) * (1.414 * np.sqrt(2.0 / (2 * OUT + 1)))
        adj = jax.random.randint(k4, (N, N), 0, 2, jnp.int32)
        return {'input': inp, 'W': W, 'a': a, 'adj': adj, 'M': N}
    _L1_gnn_all = _L1_gnn_setup()
    _L1_gnn_in = {k: v for k, v in _L1_gnn_all.items() if k in ('W', 'a', )}
    del _L1_gnn_all

    def _L2_gnn_setup():
        import jax, jax.numpy as jnp
        import numpy as np
        N = 8192
        IN_F = 128
        OUT_F = 128
        ALPHA = 0.2
        NEG_FILL = -9000000000000000.0
        key = jax.random.key(seed)
        k_adj, k_h, k_w, k_a = jax.random.split(key, 4)
        adj = jax.random.randint(k_adj, (N, N), 0, 2, dtype=jnp.int32)
        h = jax.random.normal(k_h, (N, IN_F), dtype=jnp.float32)
        W = jax.random.normal(k_w, (IN_F, OUT_F), dtype=jnp.float32) * (2.0 / (IN_F + OUT_F)) ** 0.5
        a = jax.random.normal(k_a, (2 * OUT_F, 1), dtype=jnp.float32) * (2.0 / (2 * OUT_F + 1)) ** 0.5
        return {'adj': adj, 'h': h, 'W': W, 'a': a}
    _L2_gnn_all = _L2_gnn_setup()
    _L2_gnn_in = {k: v for k, v in _L2_gnn_all.items() if k in ('W', 'a', )}
    del _L2_gnn_all

    def _L3_gnn_setup():
        import jax, jax.numpy as jnp
        import numpy as np
        NEG_INF = -1000000000.0
        key = jax.random.key(seed)
        k1, k2, k3, k4 = jax.random.split(key, 4)
        N, Fin, Fout = (8192, 128, 128)
        h = jax.random.normal(k1, (N, Fin), dtype=jnp.float32)
        adj = jax.random.randint(k2, (N, N), 0, 2, dtype=jnp.int32)
        W = jax.random.normal(k3, (Fin, Fout), dtype=jnp.float32) * (1.0 / np.sqrt(Fin))
        a = jax.random.normal(k4, (2 * Fout,), dtype=jnp.float32) * (1.0 / np.sqrt(2 * Fout))
        return {'h': h, 'adj': adj, 'W': W, 'a': a}
    _L3_gnn_all = _L3_gnn_setup()
    _L3_gnn_in = {k: v for k, v in _L3_gnn_all.items() if k in ('W', 'a', )}
    del _L3_gnn_all

    return {
        "x": x,
        "adj": adj,
        "L1_gnn_W": _L1_gnn_in["W"],
        "L1_gnn_a": _L1_gnn_in["a"],
        "L2_gnn_W": _L2_gnn_in["W"],
        "L2_gnn_a": _L2_gnn_in["a"],
        "L3_gnn_W": _L3_gnn_in["W"],
        "L3_gnn_a": _L3_gnn_in["a"],
    }

def reference(x, adj, L1_gnn_W, L1_gnn_a, L2_gnn_W, L2_gnn_a, L3_gnn_W, L3_gnn_a):
    import jax
    import jax.numpy as jnp
    def _L0_gnn_ref(X, adj):
        import jax
        import jax.numpy as jnp
        import numpy as np
        from jax import lax
        N = 8192
        F = 128
        CHUNK = 64
        neg = jnp.finfo(X.dtype).min
        mask = adj != 0
        n, f = X.shape

        def body(_, mrows):
            vals = jnp.max(jnp.where(mrows[:, :, None], X[None, :, :], neg), axis=1)
            has_nbr = jnp.any(mrows, axis=1)
            return (None, jnp.where(has_nbr[:, None], vals, jnp.zeros((), X.dtype)))
        _, out = lax.scan(body, None, mask.reshape(n // CHUNK, CHUNK, n))
        return out.reshape(n, f)

    def _L1_gnn_ref(input, W, a, adj, M):
        import jax, jax.numpy as jnp
        import numpy as np
        N = 8192
        IN = 128
        OUT = 128
        THR = 0.0001
        ALPHA = 0.2
        NEG = -1000000000.0
        h = input @ W
        a_src = a[:OUT, 0]
        a_dst = a[OUT:, 0]
        e = jax.nn.leaky_relu((h[:M] @ a_src)[:, None] + (h @ a_dst)[None, :], negative_slope=ALPHA)
        valid = (adj[:M] > 0) & (h.sum(axis=1) != 0)[None, :]
        att = jax.nn.softmax(jnp.where(valid, e, NEG), axis=1)
        att = jnp.where(valid, att, 0.0)
        L = valid.sum(axis=1).astype(h.dtype)
        top = att.max(axis=1)
        attention = jnp.where(att >= THR, att, 0.0) * L[:, None]
        attention = jnp.where((top > THR)[:, None], attention, 0.0)
        h_prime = attention @ h
        return jax.nn.elu(h[:M] + h_prime)

    def _L2_gnn_ref(adj, h, W, a):
        import jax, jax.numpy as jnp
        import numpy as np
        N = 8192
        IN_F = 128
        OUT_F = 128
        ALPHA = 0.2
        NEG_FILL = -9000000000000000.0
        Wh = h @ W
        Wh1 = Wh @ a[:OUT_F, :]
        Wh2 = Wh @ a[OUT_F:, :]
        e = jax.nn.leaky_relu(Wh1 + Wh2.T, ALPHA)
        attention = jnp.where(adj > 0, e, jnp.float32(NEG_FILL))
        attention = jax.nn.softmax(attention, axis=1)
        h_prime = attention @ Wh
        return jax.nn.elu(h_prime)

    def _L3_gnn_ref(h, adj, W, a):
        import jax, jax.numpy as jnp
        import numpy as np
        NEG_INF = -1000000000.0
        Fout = W.shape[1]
        Wh = h @ W
        a1, a2 = (a[:Fout], a[Fout:])
        s_key = Wh @ a1
        s_qry = Wh @ a2
        e = jax.nn.leaky_relu(s_qry[:, None] + s_key[None, :], negative_slope=0.2)
        scores = jnp.where(adj > 0, e, jnp.float32(NEG_INF))
        attention = jax.nn.softmax(scores, axis=1)
        h_prime = attention @ Wh
        return jax.nn.elu(h_prime)

    x = _layernorm(x + _L0_gnn_ref(x, adj), axis=-1)
    x = _layernorm(x + _L1_gnn_ref(x, L1_gnn_W, L1_gnn_a, adj, 8192), axis=-1)
    x = _layernorm(x + _L2_gnn_ref(adj, x, L2_gnn_W, L2_gnn_a), axis=-1)
    x = _layernorm(x + _L3_gnn_ref(x, adj, L3_gnn_W, L3_gnn_a), axis=-1)
    return x


_drawn_inputs = setup_inputs


def setup_inputs(seed=0):
    import zlib

    import numpy as np

    out = dict(_drawn_inputs(seed))
    spreads = {}
    factors = {}
    for name, (base, spread) in spreads.items():
        noise = np.random.default_rng([zlib.crc32(name.encode()), seed]).standard_normal(out[name].shape)
        drawn = base * np.exp(spread * noise) if base else spread * noise
        out[name] = jnp.asarray(drawn.astype(out[name].dtype))
    for name, factor in factors.items():
        out[name] = (out[name] * factor).astype(out[name].dtype)
    return out
```

```python
from contextlib import ExitStack

import concourse.bass as bass
from concourse import mybir

F32 = mybir.dt.float32
BF16 = mybir.dt.bfloat16
FP8 = mybir.dt.float8e4
I32 = mybir.dt.int32
U32 = mybir.dt.uint32
U8 = mybir.dt.uint8
ALU = mybir.AluOpType
ACT = mybir.ActivationFunctionType
AXX = mybir.AxisListType.X

P = 128
N = 8192
F = 128
T = N // P
HALF = N // 2
SEG = 128
NSEG = N // SEG
SLOTS = 64
GROUPS = 4
PER = SLOTS // GROUPS
CI = 512
NC = N // CI
TC = CI // P
TRB = 8
HT = HALF // P // TRB
BIG = 3.0e38
EPS = 1e-5
THR = 1e-4
QJ = T // 4
WR = 4


def hold(eng, sem, value):
    eng.wait_ge(sem, value)
    if not isinstance(value, int):
        eng.sem_inc(SPARE[0], 1)


SPARE = []
SEMS = []


class Phase:

    def __init__(self, nc):
        self.nc, self.all = nc, []

    def __enter__(self):
        SEMS[:] = [self.take]
        return self

    def take(self, name):
        self.all.append(self.nc.alloc_semaphore(name=name))
        return self.all[-1]

    def __exit__(self, *_):
        self.nc.all_engine_barrier()
        self.nc.clear_and_free_semaphores(self.all)
        self.nc.all_engine_barrier()


class Steps:

    def __init__(self, eng, sem, base=0):
        self.eng, self.sem, self.base, self.n = eng, sem, base, 0

    def did(self, ins):
        self.n += 1
        ins.then_inc(self.sem, 1)

    def settle(self):
        self.eng.wait_ge(self.sem, self.base + self.n)

    def do(self, ins):
        self.did(ins)
        self.settle()


class Tally:

    def __init__(self, eng, sem, start=0):
        self.eng, self.sem, self.n = eng, sem, 0
        self.reg = eng.alloc_register(f"tally_{sem.name}")
        eng.reg_mov(self.reg, start)

    def wait(self, n=1):
        self.eng.reg_add(self.reg, self.reg, n)
        hold(self.eng, self.sem, self.reg)

    def did(self, ins):
        self.n += 1
        ins.then_inc(self.sem, 1)

    def settle(self):
        n, self.n = self.n, 0
        self.wait(n)

    def do(self, ins):
        self.did(ins)
        self.settle()


def neighbour_max(nc, x, adj, mask_t, nm, deg, consts):
    ident_b, iota_b, segbase, = consts
    with ExitStack() as ctx:
        sb = lambda n, s, d: ctx.enter_context(nc.sbuf_tensor(n, s, d))
        sem = SEMS[0]
        adjb = sb("adjb", [P, 2, HALF], I32)
        maskb = sb("maskb", [P, 2, HALF], BF16)
        localb = sb("localb", [P, 2, HALF], BF16)
        stage = sb("stage", [P, T, CI], FP8)
        ring = sb("ring", [P, GROUPS, PER * F], F32)
        top = sb("top", [P, NSEG, 8], F32)
        keys = sb("keys", [P, NSEG * 8], F32)
        srt = sb("srt", [P, SLOTS], F32)
        pad = sb("pad", [P, SLOTS], F32)
        junk = sb("junk", [P, SLOTS], F32)
        idx = sb("idx", [P, 2, SLOTS], U32)
        part = sb("part", [P, GROUPS, F], F32)
        found = sb("found", [P, T], F32)
        degh = sb("degh", [P, T, 2], F32)
        miss = sb("miss", [P, T], F32)
        missed = sb("missed", [P, 1], F32)
        missed_all = sb("missed_all", [P, 1], F32)
        flag = sb("flag", [P, 1], I32)
        tp = [ctx.enter_context(nc.psum_tensor(f"tp{i}", [P, TRB, P], BF16)) for i in range(4)]

        adj_in = [sem("adj_in0"), sem("adj_in1")]
        mask_ready = sem("mask_ready")
        local_made = sem("local_made")
        transposed = sem("transposed")
        evacuated = sem("evacuated")
        stage_out = sem("stage_out")
        dve_step = sem("dve_step")
        idx_ready = sem("idx_ready")
        gathered = [sem(f"gathered{g}") for g in range(GROUPS)]
        ring_used = sem("ring_used")
        missed_ready = sem("missed_ready")
        missed_shared = sem("missed_shared")
        flag_ready = sem("flag_ready")
        fb_adj = sem("fb_adj")
        fb_adj_used = sem("fb_adj_used")
        fb_x = sem("fb_x")
        fb_step = sem("fb_step")
        nm_done = sem("nm_done")

        block = ctx.enter_context(nc.Block())
        x_rows = x
        lim = ring[:, :, :].rearrange("p g n -> p (g n)")
        FJ = 64
        xb = stage[:, :, :].rearrange("p a b -> p (a b)").bitcast(F32)
        tmp = adjb[:, :, :].rearrange("p h n -> p (h n)").bitcast(F32)

        @block.sync
        def _(sp):
            for h in range(2):
                sp.dma_start(adjb[:, h, :], adj[0:P, h * HALF:(h + 1) * HALF]).then_inc(adj_in[h], 16)
            with sp.Fori(1, T) as t:
                for h in range(2):
                    hold(sp, mask_ready, t * 2 - 1 + h)
                    sp.dma_start(adjb[:, h, :], adj[bass.ds(t * P, P), h * HALF:(h + 1) * HALF]).then_inc(adj_in[h], 16)
            sp.wait_ge(flag_ready, 1)
            more = sp.value_load(flag[0:1, 0:1], min_val=0, max_val=1)
            with sp.If(more != 0):
                with sp.Fori(0, T) as t:
                    hold(sp, fb_adj_used, t + 1)
                    sp.dma_start(adjb[:, :, :].rearrange("p h n -> p (h n)"), adj[bass.ds(t * P, P), :]).then_inc(fb_adj, 16)
                    with sp.Fori(0, N // FJ) as s:
                        hold(sp, fb_step, (t * (N // FJ) + s) * 3 + 1)
                        sp.dma_start(
                            xb[:, :].rearrange("p n -> p n"),
                            x_rows[bass.ds(s * FJ, FJ), :].rearrange("j f -> (j f)").partition_broadcast(P),
                        ).then_inc(fb_x, 16)

        @block.gpsimd
        def _(pool):
            with pool.Fori(0, T // 2) as it:
                for k in range(2):
                    hold(pool, idx_ready, it * 2 + k + 1)
                    for g in range(GROUPS):
                        hold(pool, ring_used, (it * 2 + k) * GROUPS + g + 1)
                        for s in range(PER):
                            pool.indirect_dma_start(
                                ring[:, g, s * F:(s + 1) * F], None, x_rows,
                                bass.IndirectOffsetOnAxis(ap=idx[:, k, g * PER + s:g * PER + s + 1], axis=0),
                            ).then_inc(gathered[g], 16)
            pool.wait_ge(missed_ready, 1)
            nc.gpsimd.partition_all_reduce(missed_all[:, :], missed[:, :], P, bass.bass_isa.ReduceOp.max).then_inc(missed_shared, 1)

        @block.scalar
        def _(act):
            act.sem_inc(evacuated, 4)
            act.sem_inc(stage_out, 16)
            with act.Fori(0, T // TC) as it:
                for k in range(TC):
                    t = it * TC + k
                    for h in range(2):
                        hold(act, adj_in[h], (t + 1) * 16)
                        hold(act, local_made, t * 2 + h + 1)
                        hold(act, transposed, t * 8 + (h + 1) * HT)
                        nc.scalar.activation(maskb[:, h, :], adjb[:, h, :], ACT.Sign,
                                             accum_out=degh[:, bass.ds(t, 1), h]).then_inc(mask_ready, 1)
                    if k == 0:
                        hold(act, stage_out, (it + 1) * 16)
                    for b in range(2 * HT):
                        hold(act, transposed, t * 8 + 8 + b + 1)
                        nc.scalar.activation(stage[:, b * TRB:(b + 1) * TRB, k * P:(k + 1) * P],
                                             tp[b % 4][:, :, :], ACT.Copy, saturate=False).then_inc(evacuated, 1)
                hold(act, evacuated, 4 + (it + 1) * 8 * TC)
                act.dma_start(mask_t[bass.ds(it, 1), :, :].rearrange("c p n -> p (c n)"),
                              stage[:, :, :].rearrange("p a b -> p (a b)").bitcast(U8)).then_inc(stage_out, 16)
            act.wait_ge(stage_out, (NC + 1) * 16)

        @block.tensor
        def _(pe):
            pe.sem_inc(transposed, 8)
            with pe.Fori(0, T) as t:
                for h in range(2):
                    pe.wait_ge(mask_ready, t * 2 + h + 1)
                    for b in range(HT):
                        pe.wait_ge(evacuated, t * 8 + h * HT + b + 1)
                        for i in range(TRB):
                            j = (b * TRB + i) * P
                            last = nc.tensor.transpose(tp[(h * HT + b) % 4][:, i, :], maskb[:, h, j:j + P], ident_b[:, :])
                        last.then_inc(transposed, 1)

        @block.vector
        def _(dve):
            dve.sem_inc(local_made, 2)
            dve.sem_inc(ring_used, GROUPS)
            steps = Tally(dve, dve_step)

            def extract(t, k):
                for h in range(2):
                    hold(dve, mask_ready, t * 2 + h + 1)
                    nc.vector.tensor_tensor(
                        out=localb[:, h, :].rearrange("p (s c) -> p s c", c=SEG),
                        in0=maskb[:, h, :].rearrange("p (s c) -> p s c", c=SEG),
                        in1=iota_b[:, :].unsqueeze(1).to_broadcast([P, NSEG // 2, SEG]),
                        op=ALU.mult).then_inc(local_made, 1)
                for h in range(2):
                    hold(dve, local_made, t * 2 + h + 3)
                    for s in range(NSEG // 2):
                        last = nc.vector.max(out=top[:, h * (NSEG // 2) + s, :], in_=localb[:, h, s * SEG:(s + 1) * SEG])
                steps.do(last)
                flat = top[:, :, :].rearrange("p s e -> p (s e)")
                steps.do(nc.vector.scalar_tensor_tensor(out=keys[:, :], in0=flat, scalar=0.0, in1=segbase[:, :], op0=ALU.is_gt, op1=ALU.mult))
                steps.do(nc.vector.tensor_tensor(out=keys[:, :], in0=keys[:, :], in1=flat, op=ALU.add))
                for r in range(SLOTS // 8):
                    steps.do(nc.vector.max(out=srt[:, 8 * r:8 * r + 8], in_=keys[:, :]))
                    steps.do(nc.vector.match_replace(out=keys[:, :], in_to_replace=srt[:, 8 * r:8 * r + 8], in_values=keys[:, :], imm_value=0.0))
                steps.did(nc.vector.tensor_scalar(junk[:, :], srt[:, :], 0.0, 0.0, ALU.is_gt, ALU.add, accum_out=found[:, bass.ds(t, 1)]))
                steps.do(nc.vector.tensor_scalar(pad[:, :], srt[:, :], 0.0, srt[:, 0:1], ALU.is_equal, ALU.mult))
                steps.do(nc.vector.tensor_tensor(out=pad[:, :], in0=pad[:, :], in1=srt[:, :], op=ALU.max))
                steps.did(nc.vector.tensor_scalar(idx[:, k % 2, :], pad[:, :], -1.0, 0.0, ALU.add, ALU.max))
                steps.settle()
                dve.sem_inc(idx_ready, 1)

            def reduce(t):
                for g in range(GROUPS):
                    hold(dve, gathered[g], (t + 1) * 16 * PER)
                    nc.vector.tensor_reduce(part[:, g, :], ring[:, g, :].rearrange("p (k f) -> p f k", f=F), axis=AXX,
                                            op=ALU.max).then_inc(ring_used, 1)
                hold(dve, ring_used, (t + 2) * GROUPS)
                nc.vector.tensor_reduce(nm[:, bass.ds(t, 1), :].rearrange("p o f -> p (o f)"), part[:, :, :].rearrange("p g f -> p f g"), axis=AXX,
                                        op=ALU.max).then_inc(dve_step, 1)
                steps.n += 1
                steps.settle()

            extract(0, 0)
            with dve.Fori(0, T // 2 - 1) as it:
                for k in range(2):
                    extract_at = it * 2 + k + 1
                    extract(extract_at, k + 1)
                    reduce(it * 2 + k)
            extract(T - 1, T - 1)
            reduce(T - 2)
            reduce(T - 1)
            steps.settle()
            dve.wait_ge(mask_ready, 2 * T)
            steps.do(nc.vector.tensor_tensor(out=deg[:, :], in0=degh[:, :, 0], in1=degh[:, :, 1], op=ALU.add))
            steps.do(nc.vector.tensor_tensor(out=miss[:, :], in0=deg[:, :], in1=found[:, :], op=ALU.not_equal))
            nc.vector.tensor_reduce(missed[:, :], miss[:, :], axis=AXX, op=ALU.max).then_inc(missed_ready, 1)
            dve.wait_ge(missed_shared, 1)
            nc.vector.tensor_copy(flag[:, :], missed_all[:, :]).then_inc(flag_ready, 1)
            dve.wait_ge(flag_ready, 1)
            dve.wait_ge(stage_out, (NC + 1) * 16)
            more = dve.value_load(flag[0:1, 0:1], min_val=0, max_val=1)
            with dve.If(more != 0):
                dve.sem_inc(fb_adj_used, 1)
                dve.sem_inc(fb_step, 1)
                chunks = N // FJ
                with dve.Fori(0, T) as t:
                    hold(dve, fb_adj, (t + 1) * 16)
                    nc.vector.tensor_scalar(lim, adjb[:, :, :].rearrange("p h n -> p (h n)"), 0.0, 2.0, ALU.not_equal, ALU.mult).then_inc(nm_done, 1)
                    hold(dve, nm_done, t * 3 + 1)
                    nc.vector.tensor_scalar(lim, lim, -1.0, BIG, ALU.add, ALU.mult).then_inc(nm_done, 1)
                    nc.vector.memset(part[:, 0, :], -BIG).then_inc(nm_done, 1)
                    hold(dve, nm_done, t * 3 + 3)
                    with dve.Fori(0, chunks) as s:
                        n = (t * chunks + s) * 3 + 1
                        hold(dve, fb_x, (t * chunks + s + 1) * 16)
                        nc.vector.tensor_tensor(
                            out=tmp.rearrange("p (j f) -> p j f", f=F), in0=xb.rearrange("p (j f) -> p j f", f=F),
                            in1=lim[:, bass.ds(s * FJ, FJ)].unsqueeze(2).to_broadcast([P, FJ, F]), op=ALU.min).then_inc(fb_step, 1)
                        hold(dve, fb_step, n + 1)
                        nc.vector.tensor_reduce(part[:, 1, :], tmp.rearrange("p (j f) -> p f j", f=F), axis=AXX, op=ALU.max).then_inc(fb_step, 1)
                        hold(dve, fb_step, n + 2)
                        nc.vector.tensor_tensor(out=part[:, 0, :], in0=part[:, 0, :], in1=part[:, 1, :], op=ALU.max).then_inc(fb_step, 1)
                        hold(dve, fb_step, n + 3)
                    nc.vector.tensor_copy(nm[:, bass.ds(t, 1), :].rearrange("p o f -> p (o f)"), part[:, 0, :]).then_inc(fb_adj_used, 1)
                    hold(dve, fb_adj_used, t + 2)


def first_norm(nc, x, X, deg, has, stats):
    with ExitStack() as ctx:
        sem = SEMS[0]
        bn = ctx.enter_context(nc.sbuf_tensor("bn0", [P, T, 6], F32))
        xin = ctx.enter_context(nc.sbuf_tensor("xin", [P, T, F], F32))
        x_in, step, bn_done, ag_done = sem("x_in"), sem("step0"), sem("bn_done"), sem("ag_done")
        block = ctx.enter_context(nc.Block())

        @block.sync
        def _(sp):
            sp.dma_start(xin[:, :, :], x.rearrange("(t p) f -> p t f", p=P)).then_inc(x_in, 16)

        @block.vector
        def _(dve):
            s = Steps(dve, step)
            s.do(nc.vector.tensor_scalar(has[:, :], deg[:, :], 1.0, None, ALU.min))
            s.do(nc.vector.tensor_tensor(out=X[:, :, :], in0=X[:, :, :], in1=has[:, :].unsqueeze(2).to_broadcast([P, T, F]), op=ALU.mult))
            dve.wait_ge(x_in, 16)
            s.do(nc.vector.tensor_tensor(out=X[:, :, :], in0=X[:, :, :], in1=xin[:, :, :], op=ALU.add))
            for t in range(T):
                nc.vector.bn_stats(bn[:, t, :], X[:, t, :]).then_inc(bn_done, 1)
            dve.wait_ge(bn_done, T)
            for t in range(T):
                nc.vector.bn_aggr(stats[:, t, :], bn[:, t, :]).then_inc(ag_done, 1)
            dve.wait_ge(ag_done, T)


def normalise(nc, dve, act_sqrt, sqrt_done, s, X, stats, rstd):
    s.do(nc.vector.tensor_scalar(rstd[:, :], stats[:, :, 1], EPS, None, ALU.add))
    dve.sem_inc(act_sqrt, 1)
    s.do(nc.vector.tensor_tensor(out=X[:, :, :], in0=X[:, :, :], in1=stats[:, :, 0].unsqueeze(2).to_broadcast([P, T, F]), op=ALU.subtract))
    dve.wait_ge(sqrt_done, 1)
    s.do(nc.vector.reciprocal(rstd[:, :], rstd[:, :]))
    s.do(nc.vector.tensor_tensor(out=X[:, :, :], in0=X[:, :, :], in1=rstd[:, :].unsqueeze(2).to_broadcast([P, T, F]), op=ALU.mult))


def attention_layer(nc, layer, W, a_src, a_dst, mask_t, X, has, stats, rstd, ident, lastrow, nhd, dest):
    cut = layer == 1
    with ExitStack() as ctx:
        sb = lambda n, s, d: ctx.enter_context(nc.sbuf_tensor(f"{n}_{layer}", s, d))
        names = [0]

        def sem(n):
            names[0] += 1
            return SEMS[0](f"{n}_{layer}")

        XT = sb("XT", [P, N], F32)
        GX = sb("GX", [P, T, F], F32)
        Wn = sb("Wn", [P, F], F32)
        WT = sb("WT", [P, F], F32)
        Wa = sb("Wa", [P, F + 1], F32)
        A3 = sb("A3", [P, 3], F32)
        U3 = sb("U3", [P, 3], F32)
        Urep = sb("Urep", [P, P], F32)
        sdh = sb("sdh", [P, T, 3], F32)
        dm = sb("dm", [P, 1], F32)
        D = sb("D", [P, 1], F32)
        nb = sb("nb", [P, 3], F32)
        E = sb("E", [P, T], F32)
        G = sb("G", [P, T], F32)
        zc = sb("zc", [P, 1], F32)
        mrow = sb("mrow", [1, F + 1], F32)
        cm = sb("cm", [P, P], F32)
        bn = sb("bn", [P, TC, 6], F32)
        mv = sb("mv", [P, TC, 2], F32)
        banks = [ctx.enter_context(nc.psum_tensor(f"bank{i}_{layer}", [P, 512], F32)) for i in range(8)]

        with ExitStack() as pctx:
            psem = lambda n: SEMS[0](f"{n}_{layer}")
            if cut:
                B = pctx.enter_context(nc.sbuf_tensor("B_1", [P, T], F32))
                rest = pctx.enter_context(nc.sbuf_tensor("rest_1", [P, T], F32))
            w_in, act_sqrt, sqrt_done, step = psem("w_in"), psem("act_sqrt"), psem("sqrt_done"), psem("prep_step")
            x_ready, tr, ev = psem("x_ready"), psem("tr"), psem("ev")
            wt_ps, wt_sb, u_ps, u_sb = psem("wt_ps"), psem("wt_sb"), psem("u_ps"), psem("u_sb")
            cm_sb, wa_ps = psem("cm_sb"), psem("wa_ps")
            sd_ps, dm_sb, d_all, nb_sb, egb = psem("sd_ps"), psem("dm_sb"), psem("d_all"), psem("nb_sb"), psem("egb")
            mean_sb, mean_ps = psem("mean_sb"), psem("mean_ps")
            block = pctx.enter_context(nc.Block())
            NG = T // 4

            @block.sync
            def _(sp):
                sp.dma_start(Wn[:, :], W).then_inc(w_in, 16)
                sp.dma_start(A3[:, 0:1], a_src).then_inc(w_in, 16)
                sp.dma_start(A3[:, 1:2], a_dst).then_inc(w_in, 16)

            @block.gpsimd
            def _(pool):
                pool.wait_ge(dm_sb, 1)
                nc.gpsimd.partition_all_reduce(D[:, :], dm[:, :], P, bass.bass_isa.ReduceOp.max).then_inc(d_all, 1)

            @block.tensor
            def _(pe):
                pe.wait_ge(w_in, 48)
                nc.tensor.transpose(banks[4][:, 0:P], Wn[:, :], ident[:, :]).then_inc(wt_ps, 1)
                pe.wait_ge(wt_sb, 2)
                nc.tensor.matmul(banks[5][:, 0:3], WT[:, :], A3[:, :], start=True, stop=True).then_inc(u_ps, 1)
                if not cut:
                    pe.wait_ge(cm_sb, 1)
                    nc.tensor.matmul(banks[7][:, 0:F], cm[:, :], Wn[:, :], start=True, stop=True).then_inc(wa_ps, 1)
                pe.wait_ge(x_ready, 1)
                for g in range(NG):
                    if g >= 4:
                        pe.wait_ge(ev, g - 3)
                    for k in range(4):
                        last = nc.tensor.transpose(banks[g % 4][:, k * P:(k + 1) * P], X[:, 4 * g + k, :], ident[:, :])
                    last.then_inc(tr, 1)
                pe.wait_ge(u_sb, 2)
                pe.wait_ge(ev, NG)
                for t in range(T):
                    last = nc.tensor.matmul(banks[6][:, 3 * t:3 * t + 3], XT[:, t * P:(t + 1) * P], U3[:, :], start=True, stop=True)
                last.then_inc(sd_ps, 1)
                if not cut:
                    pe.wait_ge(mean_sb, 1)
                    nc.tensor.matmul(banks[4][0:1, 0:F], zc[:, :], Wn[:, :], start=True, stop=True).then_inc(mean_ps, 1)

            @block.scalar
            def _(act):
                act.wait_ge(act_sqrt, 1)
                nc.scalar.activation(rstd[:, :], rstd[:, :], ACT.Sqrt).then_inc(sqrt_done, 1)
                for g in range(NG):
                    act.wait_ge(tr, g + 1)
                    nc.scalar.activation(XT[:, g * CI:(g + 1) * CI], banks[g % 4][:, :], ACT.Copy).then_inc(ev, 1)
                act.wait_ge(nb_sb, 1)
                nc.scalar.activation(E[:, :], sdh[:, :, 1], ACT.Exp, bias=nb[:, 0:1], scale=0.8).then_inc(egb, 1)
                nc.scalar.activation(G[:, :], sdh[:, :, 1], ACT.Exp, bias=nb[:, 1:2], scale=0.2).then_inc(egb, 1)
                if cut:
                    nc.scalar.activation(B[:, :], sdh[:, :, 1], ACT.Exp, bias=nb[:, 2:3]).then_inc(egb, 1)

            @block.vector
            def _(dve):
                s = Steps(dve, step)
                if not cut:
                    s.do(nc.vector.tensor_tensor(out=cm[:, :], in0=ident[:, :], in1=lastrow[:, :], op=ALU.subtract))
                    dve.sem_inc(cm_sb, 1)
                normalise(nc, dve, act_sqrt, sqrt_done, s, X, stats, rstd)
                dve.sem_inc(x_ready, 1)
                nc.vector.memset(A3[:, 2:3], 1.0).then_inc(wt_sb, 1)
                dve.wait_ge(wt_ps, 1)
                nc.vector.tensor_copy(WT[:, :], banks[4][:, 0:P]).then_inc(wt_sb, 1)
                dve.wait_ge(u_ps, 1)
                nc.vector.tensor_copy(U3[:, :], banks[5][:, 0:3]).then_inc(u_sb, 1)
                dve.wait_ge(u_sb, 1)
                nc.vector.tensor_copy(Urep[:, :], U3[:, 0:1].to_broadcast([P, P])).then_inc(u_sb, 1)
                if not cut:
                    dve.wait_ge(wa_ps, 1)
                    s.do(nc.vector.tensor_copy(Wa[:, 0:F], banks[7][:, 0:F]))
                    s.do(nc.vector.tensor_copy(Wa[:, F:F + 1], lastrow[:, 0:1]))
                dve.wait_ge(sd_ps, 1)
                s.do(nc.vector.tensor_copy(sdh[:, :, :].rearrange("p t c -> p (t c)"), banks[6][:, 0:3 * T]))
                nc.vector.tensor_reduce(dm[:, :], sdh[:, :, 1], axis=AXX, op=ALU.max).then_inc(dm_sb, 1)
                dve.wait_ge(d_all, 1)
                for k, r in enumerate((-0.8, -0.2, -1.0)):
                    s.did(nc.vector.tensor_scalar(nb[:, k:k + 1], D[:, :], r, None, ALU.mult))
                s.settle()
                dve.sem_inc(nb_sb, 1)
                if not cut:
                    s.do(nc.vector.tensor_reduce(zc[:, :], XT[:, :], axis=AXX, op=ALU.add))
                    s.do(nc.vector.tensor_scalar(zc[:, :], zc[:, :], 1.0 / N, None, ALU.mult))
                    dve.sem_inc(mean_sb, 1)
                dve.wait_ge(egb, 3 if cut else 2)
                if cut:
                    v = sdh[:, :, 2]
                    s.do(nc.vector.tensor_scalar(v, v, 0.0, None, ALU.not_equal))
                    s.did(nc.vector.tensor_tensor(out=G[:, :], in0=G[:, :], in1=v, op=ALU.mult))
                    s.did(nc.vector.tensor_tensor(out=B[:, :], in0=B[:, :], in1=v, op=ALU.mult))
                    s.settle()
                s.did(nc.vector.tensor_tensor(out=GX[:, :, :], in0=X[:, :, :], in1=G[:, :].unsqueeze(2).to_broadcast([P, T, F]), op=ALU.mult))
                if cut:
                    s.do(nc.vector.memset(dest["kg"][:, :, :], 0.0))
                    s.do(nc.vector.memset(dest["km"][:, :, :], 0.0))
                    for src, at, out in ((B, 0, "kg"), (G, 3, "km")):
                        s.do(nc.vector.tensor_copy(rest[:, :], src[:, :]))
                        for k in range(3):
                            part = dest[out][:, :, at + k]
                            s.do(nc.vector.tensor_copy(part, rest[:, :]))
                            s.do(nc.vector.tensor_tensor(out=rest[:, :], in0=rest[:, :], in1=part, op=ALU.subtract))
                    s.do(nc.vector.tensor_scalar(dest["kg"][:, :, 3:6], dest["km"][:, :, 3:6], -1.0, None, ALU.mult))
                    s.do(nc.vector.tensor_copy(dest["km"][:, :, 6], v))
                else:
                    s.settle()
                    s.do(nc.vector.tensor_copy(GX[:, :, F - 1], G[:, :]))
                    dve.wait_ge(mean_ps, 1)
                    s.did(nc.vector.tensor_copy(mrow[0:1, 0:F], banks[4][0:1, 0:F]))
                    s.did(nc.vector.memset(mrow[0:1, F:F + 1], 1.0))
                s.settle()

        m = sb("m", [P, 2, T, CI], FP8)
        w = sb("w", [P, WR, CI], F32)
        qb = sb("q", [P, 2, CI], F32)
        num = sb("num", [P, CI], F32)
        hp = sb("hp", [P, TC, F], F32)
        ex = sb("ex", [P, TC, F], F32)
        rd = sb("rd", [P, TC], F32)
        z = sb("z", [P, 2, CI], F32)
        nhc = None if cut else sb("nhc", [1, 2, CI], F32)
        z_ps, z_made, nh_in = sem("z_ps"), sem("z_made"), [sem("nh_in0"), sem("nh_in1")]
        if cut:
            u = sb("u", [P, 4, CI], BF16)
            den7 = sb("den7", [8, CI], F32)
            den = sb("den", [P, CI], F32)
            ratio = sb("ratio", [P, CI], F32)
            theta = sb("theta", [P, CI], F32)
        mask_in = [[sem(f"mask_in{b}{k}") for k in range(4)] for b in range(2)]
        q_ready, q_used, w_made, w_used = sem("q_ready"), sem("q_used"), sem("w_made"), sem("w_used")
        num_ready, num_used, acc_done = sem("num_ready"), sem("num_used"), sem("acc_done")
        post_ps, post_step, post_used, ex_done, mn_done = sem("post_ps"), sem("post_step"), sem("post_used"), sem("ex_done"), sem("mn_done")
        if cut:
            g_made, g_used, u_made, den_ps, den_sb, rep_ps, chain, ln_done, th_done, rep_used = (
                sem(n) for n in ("g_made", "g_used", "u_made", "den_ps", "den_sb", "rep_ps", "chain", "ln_done", "th_done", "rep_used"))
        block = ctx.enter_context(nc.Block())
        acc = banks[0:2]
        hb = banks[2:4]
        PO = CI // 2
        made = [0]

        def chunks(eng, chunk, end, say_last=False):
            chunk(0, 0, True)
            with eng.Fori(0, NC // 2 - 1) as it:
                chunk(it * 2 + 1, 1, False)
                chunk(it * 2 + 2, 0, False)
            if say_last:
                chunk(NC - 1, 1, False, True)
            else:
                chunk(NC - 1, 1, False)
            end(NC - 1, 1)

        @block.sync
        def _(sp):
            def load(c, b, k):
                src = mask_t[bass.ds(c, 1), :, :].rearrange("c p (t n) -> p (c t) n", n=CI)
                sp.dma_start(m[:, b, k * QJ:(k + 1) * QJ, :].bitcast(U8), src[:, k * QJ:(k + 1) * QJ, :]).then_inc(mask_in[b][k], 16)

            for b in range(2):
                for k in range(4):
                    load(b, b, k)
            with sp.Fori(0, NC // 2 - 1) as it:
                for b in range(2):
                    for k in range(4):
                        hold(sp, w_made, (it * 2 + b) * T + (k + 1) * QJ)
                        load(it * 2 + b + 2, b, k)

        if not cut:
            @block.gpsimd
            def _(pool):
                def load(c, b):
                    pool.dma_start(nhc[0:1, b, :], nhd[:, bass.ds(c * CI, CI)]).then_inc(nh_in[b], 16)

                for b in range(2):
                    load(b, b)
                with pool.Fori(0, NC // 2 - 1) as it:
                    for b in range(2):
                        hold(pool, post_ps, it * 2 + b + 1)
                        load(it * 2 + b + 2, b)

        @block.tensor
        def _(pe):
            def row_terms(c):
                if cut:
                    pe.wait_ge(rep_used, c + 1)
                nc.tensor.matmul(banks[7][:, :], Urep[:, :], XT[:, bass.ds(c * CI, CI)], start=True, stop=True).then_inc(z_ps, 1)

            def post(c, b):
                if not cut:
                    pe.wait_ge(nh_in[b], (c - b + 2) * 8)
                pe.wait_ge(num_ready, c + 1)
                pe.wait_ge(post_used, c + 1)
                for k in range(TC):
                    out = hb[k // 2]
                    o = (k % 2) * PO
                    lhs = num[:, k * P:(k + 1) * P]
                    if cut:
                        last = nc.tensor.matmul(out[:, o:o + F], lhs, Wn[:, :], start=True, stop=True)
                    else:
                        nc.tensor.matmul(out[:, o:o + F + 1], lhs, Wa[:, :], start=True, stop=False)
                        last = nc.tensor.matmul(out[:, o:o + F + 1], nhc[0:1, b, k * P:(k + 1) * P], mrow[0:1, :], start=False, stop=True)
                last.then_inc(post_ps, 1)

            def chunk(c, b, first, last_chunk=False):
                if first:
                    row_terms(0)
                if cut:
                    for j in range(T):
                        if j == 24 and not first:
                            post(c - 1, 1 - b)
                        g_in_order.wait()
                        nc.tensor.matmul(banks[4][0:8, :], dest["kg"][:, j, :], u[:, j % 4, :], start=(j == 0), stop=False)
                        nc.tensor.matmul(banks[4][0:8, :], dest["km"][:, j, :], m[:, b, j, :], start=False, stop=(j == T - 1)).then_inc(g_used, 1)
                    pe.wait_ge(den_sb, c + 1)
                    pe.wait_ge(z_made, c + 1)
                    for k in range(3):
                        last = nc.tensor.matmul(banks[5 + k][:, :], dest["sel"][0:8, k, :], den7[:, :], start=True, stop=True)
                    last.then_inc(rep_ps, 1)
                for j in range(T):
                    if j == 8 and not first and not cut:
                        post(c - 1, 1 - b)
                    if j == 32 and not last_chunk:
                        row_terms(c + 1)
                    w_in_order.wait()
                    last = nc.tensor.matmul(acc[b][:, :], GX[:, j, :], w[:, j % WR, :], start=(j == 0), stop=(j == T - 1))
                    last.then_inc(w_used, 1)

            w_in_order = Tally(pe, w_made)
            g_in_order = Tally(pe, g_made) if cut else None
            chunks(pe, chunk, post, True)

        @block.scalar
        def _(act):
            def take(c, b):
                hold(act, w_used, WR + (c + 1) * T)
                hold(act, num_used, c + 1)
                if not cut:
                    nc.scalar.activation(num[:, :], acc[b][:, :], ACT.Copy).then_inc(num_ready, 1)

            def expo(c):
                hold(act, mn_done, c + 1)
                nc.scalar.activation(ex[:, :, :], ex[:, :, :], ACT.Exp).then_inc(ex_done, 1)

            def chunk(c, b, first):
                hold(act, q_used, c + 1)
                hold(act, z_ps, c + 1)
                nc.scalar.activation(z[:, b, :], banks[7][:, :], ACT.Relu, bias=D[:, 0:1]).then_inc(z_made, 1)
                hold(act, z_made, c + 1)
                nc.scalar.activation(qb[:, b, :], z[:, b, :], ACT.Exp, scale=-0.8).then_inc(q_ready, 1)
                if cut:
                    if not first:
                        expo(c - 1)
                    hold(act, g_used, 4 + (c + 1) * T)
                    nc.scalar.activation(den7[:, :], banks[4][0:8, :], ACT.Copy).then_inc(den_sb, 1)
                    hold(act, chain, c * 8 + 3)
                    nc.scalar.activation(theta[:, :], den[:, :], ACT.Ln, scale=THR).then_inc(ln_done, 1)
                    hold(act, chain, c * 8 + 8)
                    nc.scalar.activation(theta[:, :], theta[:, :], ACT.Exp).then_inc(th_done, 1)
                elif not first:
                    take(c - 1, 1 - b)
                    expo(c - 1)

            def end(c, b):
                if not cut:
                    take(c, b)
                expo(c)

            chunks(act, chunk, end)

        @block.vector
        def _(dve):
            dve.sem_inc(post_used, 1)
            dve.sem_inc(num_used, 1)
            if cut:
                dve.sem_inc(rep_used, 1)
                dve.sem_inc(g_used, 4)
            dve.sem_inc(w_used, WR)
            dve.sem_inc(q_used, 2)
            w_free = Tally(dve, w_used)
            post_steps = Tally(dve, post_step)
            if cut:
                g_free, u_done, chain_steps = Tally(dve, g_used), Tally(dve, u_made), Tally(dve, chain)

            def scale_sums(c, b):
                hold(dve, w_used, WR + (c + 1) * T)
                s = post_steps
                s.do(nc.vector.tensor_tensor(out=num[:, :], in0=acc[b][:, :], in1=ratio[:, :], op=ALU.mult))
                s.did(nc.vector.tensor_tensor(out=num[:, :], in0=num[:, :], in1=XT[:, bass.ds(c * CI, CI)], op=ALU.add))
                s.settle()
                dve.sem_inc(num_ready, 1)

            def post(c, b):
                hold(dve, post_ps, c + 1)
                dve.sem_inc(num_used, 1)
                s = post_steps
                raw = [hb[k // 2][:, (k % 2) * PO:(k % 2) * PO + F + 1] for k in range(TC)]
                if cut:
                    for k in range(2):
                        s.did(nc.vector.tensor_copy(hp[:, 2 * k:2 * k + 2, :], hb[k][:, :].rearrange("p (a n) -> p a n", a=2)[:, :, 0:F]))
                    s.settle()
                else:
                    for k in range(2):
                        s.did(nc.vector.reciprocal(rd[:, 2 * k:2 * k + 2], hb[k][:, :].rearrange("p (a n) -> p a n", a=2)[:, :, F]))
                    s.settle()
                    for k in range(2):
                        s.did(nc.vector.tensor_tensor(out=hp[:, 2 * k:2 * k + 2, :], in0=hb[k][:, :].rearrange("p (a n) -> p a n", a=2)[:, :, 0:F],
                                                      in1=rd[:, 2 * k:2 * k + 2].unsqueeze(2).to_broadcast([P, 2, F]), op=ALU.mult))
                    s.settle()
                dve.sem_inc(post_used, 1)
                nc.vector.tensor_scalar(ex[:, :, :], hp[:, :, :], 0.0, None, ALU.min).then_inc(mn_done, 1)
                hold(dve, ex_done, c + 1)
                s.do(nc.vector.scalar_tensor_tensor(out=hp[:, :, :], in0=hp[:, :, :], scalar=0.0, in1=ex[:, :, :], op0=ALU.max, op1=ALU.add))
                xc = X[:, bass.ds(c * TC, TC), :]
                s.do(nc.vector.scalar_tensor_tensor(out=xc, in0=hp[:, :, :], scalar=-1.0, in1=xc, op0=ALU.add, op1=ALU.add))
                for k in range(TC):
                    last = nc.vector.bn_stats(bn[:, k, :], X[:, bass.ds(c * TC + k, 1), :].rearrange("p o f -> p (o f)"))
                s.do(last)
                for k in range(TC):
                    last = nc.vector.bn_aggr(mv[:, k, :], bn[:, k, :])
                s.do(last)
                s.do(nc.vector.tensor_copy(stats[:, bass.ds(c * TC, TC), :], mv[:, :, :]))

            def chunk(c, b, first):
                q = qb[:, b, :]
                hold(dve, q_ready, c + 1)
                if cut:
                    for j in range(T):
                        if j % QJ == 0:
                            hold(dve, mask_in[b][j // QJ], wait_of(c, b))
                        g_free.wait()
                        nc.vector.scalar_tensor_tensor(out=u[:, j % 4, :], in0=q, scalar=E[:, j:j + 1], in1=m[:, b, j, :],
                                                       op0=ALU.is_lt, op1=ALU.mult).then_inc(g_made, 1)
                        if j == 16 and not first:
                            scale_sums(c - 1, 1 - b)
                        if j == 32 and not first:
                            post(c - 1, 1 - b)
                    hold(dve, rep_ps, c + 1)
                    s = chain_steps
                    s.do(nc.vector.tensor_tensor(out=den[:, :], in0=banks[6][:, :], in1=q, op=ALU.mult))
                    s.do(nc.vector.tensor_tensor(out=den[:, :], in0=den[:, :], in1=banks[5][:, :], op=ALU.add))
                    s.do(nc.vector.tensor_scalar(den[:, :], den[:, :], 1e-30, None, ALU.max))
                    s.do(nc.vector.reciprocal(ratio[:, :], den[:, :]))
                    s.do(nc.vector.tensor_tensor(out=ratio[:, :], in0=ratio[:, :], in1=banks[7][:, :], op=ALU.mult))
                    dve.sem_inc(rep_used, 1)
                    hold(dve, ln_done, c + 1)
                    s.do(nc.vector.scalar_tensor_tensor(out=den[:, :], in0=z[:, b, :], scalar=0.8, in1=theta[:, :], op0=ALU.mult, op1=ALU.add))
                    s.do(nc.vector.tensor_scalar(den[:, :], den[:, :], 4.0, None, ALU.mult))
                    s.do(nc.vector.scalar_tensor_tensor(out=theta[:, :], in0=theta[:, :], scalar=0.8, in1=den[:, :], op0=ALU.mult, op1=ALU.min))
                    hold(dve, th_done, c + 1)

                    def keep(j):
                        nc.vector.scalar_tensor_tensor(out=u[:, j % 4, :], in0=theta[:, :], scalar=E[:, j:j + 1], in1=m[:, b, j, :],
                                                       op0=ALU.is_le, op1=ALU.mult).then_inc(u_made, 1)

                    keep(0)
                    for j in range(T):
                        if j + 1 < T:
                            keep(j + 1)
                        u_done.wait()
                        w_free.wait()
                        nc.vector.scalar_tensor_tensor(out=w[:, j % WR, :], in0=q, scalar=E[:, j:j + 1], in1=u[:, j % 4, :],
                                                       op0=ALU.max, op1=ALU.mult).then_inc(w_made, 1)
                else:
                    for j in range(T):
                        if j % QJ == 0:
                            hold(dve, mask_in[b][j // QJ], wait_of(c, b))
                        w_free.wait()
                        nc.vector.scalar_tensor_tensor(out=w[:, j % WR, :], in0=q, scalar=E[:, j:j + 1], in1=m[:, b, j, :],
                                                       op0=ALU.max, op1=ALU.mult).then_inc(w_made, 1)
                        if j == 24 and not first:
                            post(c - 1, 1 - b)
                hold(dve, w_made, (c + 1) * T)
                dve.sem_inc(q_used, 1)

            def wait_of(c, b):
                return (c - b + 2) * 8

            def end(c, b):
                if cut:
                    scale_sums(c, b)
                post(c, b)

            chunks(dve, chunk, end)


def program(nc, x, adj, W1, a1, W2, a2, W3, a3, out):
    mask_t = nc.dram_tensor("mask_t", [NC, P, T * CI], U8, kind="Internal").ap()
    nhd = nc.dram_tensor("nhd", [1, N], F32, kind="Internal").ap()
    with ExitStack() as ctx:
        SPARE[:] = [ctx.enter_context(nc.semaphore("spare"))]
        sb = lambda n, s, d: ctx.enter_context(nc.sbuf_tensor(n, s, d))
        X = sb("X", [P, T, F], F32)
        ident = sb("ident", [P, P], F32)
        lastrow = sb("lastrow", [P, P], F32)
        deg = sb("deg", [P, T], F32)
        has = sb("has", [P, T], F32)
        nohas = sb("nohas", [P, T], F32)
        nhT = sb("nhT", [T, P], F32)
        stats = sb("stats", [P, T, 2], F32)
        rstd = sb("rstd", [P, T], F32)
        kg = sb("kg", [P, T, 8], BF16)
        km = sb("km", [P, T, 8], BF16)
        sel = sb("sel", [8, 3, P], F32)

        with Phase(nc), ExitStack() as c0:
            sb0 = lambda n, s, d: c0.enter_context(nc.sbuf_tensor(n, s, d))
            ident_b = sb0("ident_b", [P, P], BF16)
            iota_i = sb0("iota_i", [P, NSEG * 8], I32)
            iota_b = sb0("iota_b", [P, SEG], BF16)
            segbase = sb0("segbase", [P, NSEG * 8], F32)
            with ExitStack() as c1:
                made, used, again = (SEMS[0](n) for n in ("made", "used", "again"))
                block = c1.enter_context(nc.Block())

                @block.gpsimd
                def _(pool):
                    s = Steps(pool, made)
                    s.do(nc.gpsimd.memset(ident[:, :], 0.0))
                    s.do(nc.gpsimd.affine_select(out=ident[:, :], in_=ident[:, :], compare_op=ALU.not_equal, fill=1.0, base=0, pattern=[[-1, P]], channel_multiplier=1))
                    s.do(nc.gpsimd.memset(lastrow[:, :], 0.0))
                    s.do(nc.gpsimd.affine_select(out=lastrow[:, :], in_=lastrow[:, :], compare_op=ALU.not_equal, fill=1.0, base=-(P - 1), pattern=[[0, P]], channel_multiplier=1))
                    s.do(nc.gpsimd.iota(iota_i[:, 0:SEG], pattern=[[1, SEG]], base=1, channel_multiplier=0))
                    pool.wait_ge(used, 2)
                    s.do(nc.gpsimd.iota(iota_i[:, :], pattern=[[SEG, NSEG], [0, 8]], base=0, channel_multiplier=0))
                    s.do(nc.gpsimd.memset(sel[:, :, :], 1.0))
                    for k in range(3):
                        s.do(nc.gpsimd.affine_select(out=sel[:, k, :], in_=sel[:, k, :], compare_op=ALU.is_ge, fill=0.0, base=-3 * k, pattern=[[0, P]], channel_multiplier=1))
                        hi = (2, 5, 6)[k]
                        s.do(nc.gpsimd.affine_select(out=sel[:, k, :], in_=sel[:, k, :], compare_op=ALU.is_ge, fill=0.0, base=hi, pattern=[[0, P]], channel_multiplier=-1))

                @block.vector
                def _(dve):
                    dve.wait_ge(made, 5)
                    nc.vector.tensor_copy(ident_b[:, :], ident[:, :]).then_inc(used, 1)
                    nc.vector.tensor_copy(iota_b[:, :], iota_i[:, 0:SEG]).then_inc(used, 1)
                    dve.wait_ge(made, 6)
                    nc.vector.tensor_copy(segbase[:, :], iota_i[:, :]).then_inc(again, 1)
                    dve.wait_ge(again, 1)

            neighbour_max(nc, x, adj, mask_t, X, deg, (ident_b, iota_b, segbase))
            first_norm(nc, x, X, deg, has, stats)

        with Phase(nc), ExitStack() as c2:
            tps = c2.enter_context(nc.psum_tensor("tps", [T, P], F32))
            a, b, c, d = (SEMS[0](n) for n in ("nh_a", "nh_b", "nh_c", "nh_d"))
            block = c2.enter_context(nc.Block())

            @block.vector
            def _(dve):
                nc.vector.tensor_scalar(nohas[:, :], has[:, :], -1.0, 1.0, ALU.mult, ALU.add).then_inc(a, 1)
                dve.wait_ge(b, 1)
                nc.vector.tensor_copy(nhT[:, :], tps[:, :]).then_inc(c, 1)

            @block.tensor
            def _(pe):
                pe.wait_ge(a, 1)
                nc.tensor.transpose(tps[:, :], nohas[:, :], ident[:, :]).then_inc(b, 1)

            @block.sync
            def _(sp):
                sp.wait_ge(c, 1)
                sp.dma_start(nhd.rearrange("o (t p) -> (o t) p", p=P), nhT[:, :]).then_inc(d, 16)
                sp.wait_ge(d, 16)

        dest = {"kg": kg, "km": km, "sel": sel}
        with Phase(nc):
            attention_layer(nc, 1, W1, a1[0:F, :], a1[F:2 * F, :], mask_t, X, has, stats, rstd, ident, lastrow, nhd, dest)
        with Phase(nc):
            attention_layer(nc, 2, W2, a2[0:F, :], a2[F:2 * F, :], mask_t, X, has, stats, rstd, ident, lastrow, nhd, dest)
        with Phase(nc):
            attention_layer(nc, 3, W3, a3[F:2 * F, :], a3[0:F, :], mask_t, X, has, stats, rstd, ident, lastrow, nhd, dest)

        with Phase(nc), ExitStack() as c3:
            step, want, got, done, ready = (SEMS[0](n) for n in ("fstep", "want", "got", "written", "ready"))
            block = c3.enter_context(nc.Block())

            @block.vector
            def _(dve):
                normalise(nc, dve, want, got, Steps(dve, step), X, stats, rstd)
                dve.sem_inc(ready, 1)

            @block.scalar
            def _(act):
                act.wait_ge(want, 1)
                nc.scalar.activation(rstd[:, :], rstd[:, :], ACT.Sqrt).then_inc(got, 1)

            @block.sync
            def _(sp):
                sp.wait_ge(ready, 1)
                sp.dma_start(out.rearrange("(t p) f -> p t f", p=P), X[:, :, :]).then_inc(done, 16)
                sp.wait_ge(done, 16)


_INS = ["x", "adj", "L1_gnn_W", "L1_gnn_a", "L2_gnn_W", "L2_gnn_a", "L3_gnn_W", "L3_gnn_a"]


def kernel(**inputs):
    import numpy as np
    import concourse.bacc as bacc
    from concourse.bass_utils import run_bass_kernel_spmd

    nc = bacc.Bacc("TRN2", target_bir_lowering=False, num_devices=1)
    arrays, args = {}, []
    for name in _INS:
        a = np.ascontiguousarray(inputs[name])
        if a.ndim == 1:
            a = a.reshape(-1, 1)
        arrays[f"in_{name}"] = a
        args.append(nc.dram_tensor(f"in_{name}", a.shape, mybir.dt.from_np(a.dtype), kind="ExternalInput").ap())
    out = nc.dram_tensor("out", (N, F), F32, kind="ExternalOutput").ap()
    program(nc, *args, out)
    r = run_bass_kernel_spmd(nc, [arrays], core_ids=[0])
    return r.results[0]["out"]
```

```python
from contextlib import ExitStack

import concourse.bass as bass
from concourse import mybir

F32 = mybir.dt.float32
BF16 = mybir.dt.bfloat16
FP8 = mybir.dt.float8e4
I32 = mybir.dt.int32
U32 = mybir.dt.uint32
U8 = mybir.dt.uint8
ALU = mybir.AluOpType
ACT = mybir.ActivationFunctionType
AXX = mybir.AxisListType.X

P = 128
N = 8192
F = 128
T = N // P
HALF = N // 2
WORD = 16
WPG = P // WORD
NW = N // WORD
EXPONENT = 0x7F800000
MORE = 8
DEEP = 4
SLOTS = 36
SIZES = (8, 8, 8, 4, 4, 4)
GROUPS = len(SIZES)
FIRST = [sum(SIZES[:g]) for g in range(GROUPS)]
SURE = 3
SRT = (SLOTS + 7) // 8 * 8
CI = 512
NC = N // CI
TC = CI // P
TRB = 8
HT = HALF // P // TRB
BIG = 3.0e38
EPS = 1e-5
THR = 1e-4
TINY = 1e-30
QJ = T // 4
RATIOS_AT = 56
SPREAD_AT = 54
CHAIN = 2
WR = 4
AR = 4
EXPO_AT = 46


def hold(eng, sem, value):
    eng.wait_ge(sem, value)
    if not isinstance(value, int):
        eng.sem_inc(SPARE[0], 1)


SPARE = []
SEMS = []


class Phase:

    def __init__(self, nc):
        self.nc, self.all = nc, []

    def __enter__(self):
        SEMS[:] = [self.take]
        return self

    def take(self, name):
        self.all.append(self.nc.alloc_semaphore(name=name))
        return self.all[-1]

    def __exit__(self, *_):
        self.nc.all_engine_barrier()
        self.nc.clear_and_free_semaphores(self.all)
        self.nc.all_engine_barrier()


class Steps:

    def __init__(self, eng, sem, base=0):
        self.eng, self.sem, self.base, self.n = eng, sem, base, 0

    def did(self, ins):
        self.n += 1
        ins.then_inc(self.sem, 1)

    def settle(self):
        self.eng.wait_ge(self.sem, self.base + self.n)

    def do(self, ins):
        self.did(ins)
        self.settle()


class Tally:

    def __init__(self, eng, sem, start=0):
        self.eng, self.sem, self.n = eng, sem, 0
        self.reg = eng.alloc_register(f"tally_{sem.name}")
        eng.reg_mov(self.reg, start)

    def wait(self, n=1):
        self.eng.reg_add(self.reg, self.reg, n)
        hold(self.eng, self.sem, self.reg)

    def did(self, ins):
        self.n += 1
        ins.then_inc(self.sem, 1)

    def settle(self):
        n, self.n = self.n, 0
        self.wait(n)

    def do(self, ins):
        self.did(ins)
        self.settle()


def neighbour_max(nc, x, adj, mask_t, x_ext, nm, deg, consts):
    ident_b, powers, code_no = consts
    with ExitStack() as ctx:
        sb = lambda n, s, d: ctx.enter_context(nc.sbuf_tensor(n, s, d))
        sem = SEMS[0]
        adjb = sb("adjb", [P, 2, HALF], I32)
        maskb = sb("maskb", [P, 2, HALF], BF16)
        stage = sb("stage", [P, T, CI], FP8)
        ring = sb("ring", [P, SLOTS, F], F32)
        xs = sb("xs", [P, 3, T, F], BF16)
        codes = sb("codes", [P, NW], F32)
        high = sb("high", [P, NW], F32)
        keys = sb("keys", [P, NW + (DEEP - 1) * MORE], F32)
        many = sb("many", [P, MORE], F32)
        many_no = sb("many_no", [P, MORE], I32)
        many_high = sb("many_high", [P, MORE], F32)
        srt = sb("srt", [P, SRT], F32)
        bit = sb("bit", [P, SRT], I32)
        base = sb("base", [P, SRT], I32)
        pad = sb("pad", [P, SRT], F32)
        junk = sb("junk", [P, T], F32)
        idx = sb("idx", [P, 2, SRT], U32)
        part = sb("part", [P, GROUPS + T // 8, F], F32)
        need = sb("need", [P, 2, 4], BF16)
        need_i = sb("need_i", [1, 2, 4], I32)
        pen = sb("pen", [P, 2, T], BF16)
        pen_t = sb("pen_t", [T, 2, P], BF16)
        counts = sb("counts", [P, T], F32)
        several = sb("several", [P, T], F32)
        found = sb("found", [P, T], F32)
        due = sb("due", [P, T], F32)
        missed = sb("missed", [P, 1], F32)
        missed_all = sb("missed_all", [P, 1], F32)
        flag = sb("flag", [P, 1], I32)
        ones = sb("ones", [P, 1], BF16)
        tp = [ctx.enter_context(nc.psum_tensor(f"tp{i}", [P, TRB, P], BF16)) for i in range(2)]
        cnt = ctx.enter_context(nc.psum_tensor("cnt", [P, T], F32))
        code_ps = ctx.enter_context(nc.psum_tensor("code_ps", [P, T, WPG], F32))
        pen_ps = tp[0][0:T, 0, :]
        need_ps = tp[0][0:1, 1, 0:8].bitcast(F32)
        sums = [ctx.enter_context(nc.psum_tensor(f"sums{i}", [P, 8, F], F32)) for i in range(2)]

        x_in = sem("x_in")
        x_copied = sem("x_copied")
        split = sem("split")
        low_ready = sem("low_ready")
        low_in = sem("low_in")
        adj_in = [sem("adj_in0"), sem("adj_in1")]
        mask_ready = sem("mask_ready")
        transposed = sem("transposed")
        evacuated = sem("evacuated")
        stage_out = sem("stage_out")
        counted = sem("counted")
        cnt_used = sem("cnt_used")
        pen_ready = sem("pen_ready")
        need_made = sem("need_made")
        need_in = sem("need_in")
        pen_turned = sem("pen_turned")
        pen_in = sem("pen_in")
        sums_ready = sem("sums_ready")
        sums_used = sem("sums_used")
        dve_step = sem("dve_step")
        idx_ready = sem("idx_ready")
        gathered = [sem(f"gathered{g}") for g in range(SURE)]
        blanked = sem("blanked")
        rest_ready = sem("rest_ready")
        ring_used = sem("ring_used")
        missed_ready = sem("missed_ready")
        missed_shared = sem("missed_shared")
        flag_ready = sem("flag_ready")
        fb_adj = sem("fb_adj")
        fb_adj_used = sem("fb_adj_used")
        fb_x = sem("fb_x")
        fb_step = sem("fb_step")
        nm_done = sem("nm_done")

        block = ctx.enter_context(nc.Block())
        lim = xs[:, :, :, :].rearrange("p k t f -> p (k t f)").bitcast(F32)[:, 0:N]
        FJ = 64
        xb = stage[:, :, :].rearrange("p a b -> p (a b)").bitcast(F32)
        tmp = adjb[:, :, :].rearrange("p h n -> p (h n)").bitcast(F32)

        @block.sync
        def _(sp):
            sp.dma_start(nm[:, :, :], x.rearrange("(t p) f -> p t f", p=P)).then_inc(x_in, 16)
            for h in range(2):
                sp.dma_start(adjb[:, h, :], adj[0:P, h * HALF:(h + 1) * HALF]).then_inc(adj_in[h], 16)
            with sp.Fori(1, T) as t:
                for h in range(2):
                    hold(sp, mask_ready, t * 2 - 1 + h)
                    sp.dma_start(adjb[:, h, :], adj[bass.ds(t * P, P), h * HALF:(h + 1) * HALF]).then_inc(adj_in[h], 16)
            sp.wait_ge(flag_ready, 1)
            more = sp.value_load(flag[0:1, 0:1], min_val=0, max_val=1)
            with sp.If(more != 0):
                with sp.Fori(0, T) as t:
                    hold(sp, fb_adj_used, t + 1)
                    sp.dma_start(adjb[:, :, :].rearrange("p h n -> p (h n)"), adj[bass.ds(t * P, P), :]).then_inc(fb_adj, 16)
                    with sp.Fori(0, N // FJ) as s:
                        hold(sp, fb_step, (t * (N // FJ) + s) * 3 + 1)
                        sp.dma_start(
                            xb, x[bass.ds(s * FJ, FJ), :].rearrange("j f -> (j f)").partition_broadcast(P),
                        ).then_inc(fb_x, 16)

        @block.gpsimd
        def _(pool):
            pool.dma_start(x_ext[0:N, :], x).then_inc(x_copied, 16)
            pool.wait_ge(low_ready, 1)
            pool.dma_start(x_ext[N:N + 1, :], part[0:1, 0, :]).then_inc(low_in, 16)
            pool.wait_ge(x_copied, 16)
            pool.wait_ge(low_in, 16)
            blanks = Tally(pool, blanked, 1)
            extra = Tally(pool, low_in, 16)
            pool.sem_inc(blanked, 1)

            def gather(k, g, done):
                for s in range(FIRST[g], FIRST[g] + SIZES[g]):
                    pool.indirect_dma_start(ring[:, s, :], None, x_ext,
                                            bass.IndirectOffsetOnAxis(ap=idx[:, k, s:s + 1], axis=0)).then_inc(done, 16)

            def rest_in():
                extra.wait(0)
                blanks.wait(0)
                pool.sem_inc(rest_ready, 1)

            def tile(t, k, first=False):
                hold(pool, idx_ready, t + 1)
                for g in range(SURE):
                    hold(pool, ring_used, t * GROUPS + g + 1)
                    gather(k, g, gathered[g])
                    if g == 0 and not first:
                        rest_in()
                hold(pool, need_in, t + 1)
                for g in range(SURE, GROUPS):
                    hold(pool, ring_used, t * GROUPS + g + 1)
                    rows = pool.value_load(need_i[0:1, k, g - SURE:g - SURE + 1], min_val=0, max_val=P)
                    with pool.If(rows != 0):
                        gather(k, g, low_in)
                        pool.reg_add(extra.reg, extra.reg, 16 * SIZES[g])
                    with pool.If(rows == 0):
                        nc.gpsimd.memset(ring[:, FIRST[g]:FIRST[g] + SIZES[g], :], -BIG).then_inc(blanked, 1)
                        pool.reg_add(blanks.reg, blanks.reg, 1)

            tile(0, 0, True)
            with pool.Fori(0, T // 2 - 1) as it:
                tile(it * 2 + 1, 1)
                tile(it * 2 + 2, 0)
            tile(T - 1, 1)
            rest_in()
            pool.wait_ge(missed_ready, 1)
            nc.gpsimd.partition_all_reduce(missed_all[:, :], missed[:, :], P, bass.bass_isa.ReduceOp.max).then_inc(missed_shared, 1)

        @block.scalar
        def _(act):
            act.sem_inc(evacuated, 2)
            act.sem_inc(stage_out, 16)

            def turn_in(t, k):
                hold(act, pen_turned, t + 1)
                nc.scalar.activation(need_i[0:1, k % 2, :], need_ps, ACT.Copy).then_inc(need_in, 1)
                nc.scalar.activation(pen_t[:, k % 2, :], pen_ps, ACT.Copy).then_inc(pen_in, 1)

            def stages(it, first):
                for k in range(TC):
                    t = it * TC + k
                    for h in range(2):
                        hold(act, adj_in[h], (t + 1) * 16)
                        hold(act, transposed, t * 8 + (h + 1) * HT)
                        nc.scalar.activation(maskb[:, h, :], adjb[:, h, :], ACT.Sign).then_inc(mask_ready, 1)
                    if k == 0:
                        hold(act, stage_out, (it + 1) * 16)
                    for b in range(2 * HT):
                        hold(act, transposed, t * 8 + 8 + b + 1)
                        nc.scalar.activation(stage[:, b * TRB:(b + 1) * TRB, k * P:(k + 1) * P],
                                             tp[b % 2][:, :, :], ACT.Copy, saturate=False).then_inc(evacuated, 1)
                    if k or not first:
                        turn_in(t - 1, k - 1)
                hold(act, evacuated, 2 + (it + 1) * 8 * TC)
                act.dma_start(mask_t[bass.ds(it, 1), :, :].rearrange("c p n -> p (c n)"),
                              stage[:, :, :].rearrange("p a b -> p (a b)").bitcast(U8)).then_inc(stage_out, 16)

            stages(0, True)
            with act.Fori(1, T // TC) as it:
                stages(it, False)
            turn_in(T - 1, T - 1)
            act.wait_ge(stage_out, (NC + 1) * 16)

        @block.tensor
        def _(pe):
            pe.sem_inc(transposed, 8)
            pe.wait_ge(split, 5)

            def sum_groups(t, k):
                hold(pe, pen_ready, t + 1)
                hold(pe, need_made, t + 1)
                nc.tensor.matmul(need_ps, ones[:, :], need[:, k % 2, :], start=True, stop=True)
                nc.tensor.transpose(pen_ps, pen[:, k % 2, :], ident_b[:, :]).then_inc(pen_turned, 1)
                pe.wait_ge(pen_in, t + 1)
                for e in range(T // 8):
                    pe.wait_ge(sums_used, t * (T // 8) + e + 1)
                    for half in range(2):
                        g0 = 8 * e + 4 * half
                        nc.tensor.matmul(sums[e % 2][:, 4 * half:4 * half + 4, :].rearrange("p g f -> p (g f)"), pen_t[:, k % 2, :],
                                         ident_b[0:T, g0:g0 + 4].unsqueeze(2).to_broadcast([T, 4, F]), start=True, stop=False, skip_group_check=True)
                        for g in range(4):
                            for part_ in range(3):
                                last = nc.tensor.matmul(sums[e % 2][:, 4 * half + g, :], stage[:, g0 + g, k * P:(k + 1) * P], xs[:, part_, g0 + g, :],
                                                        start=False, stop=(part_ == 2), skip_group_check=True)
                    last.then_inc(sums_ready, 1)

            def tiles(it, first):
                for k in range(TC):
                    t = it * TC + k
                    for h in range(2):
                        pe.wait_ge(mask_ready, t * 2 + h + 1)
                        for b in range(HT):
                            pe.wait_ge(evacuated, t * 8 + h * HT + b + 1)
                            for i in range(TRB):
                                j = (b * TRB + i) * P
                                last = nc.tensor.transpose(tp[(h * HT + b) % 2][:, i, :], maskb[:, h, j:j + P], ident_b[:, :])
                            last.then_inc(transposed, 1)
                    hold(pe, evacuated, t * 8 + 8 + 2)
                    hold(pe, cnt_used, t + 1)
                    for g in range(T):
                        nc.tensor.matmul(cnt[:, g:g + 1], stage[:, g, k * P:(k + 1) * P], ones[:, :], start=True, stop=True)
                        last = nc.tensor.matmul(code_ps[:, g, :], stage[:, g, k * P:(k + 1) * P], powers[:, :], start=True, stop=True)
                    last.then_inc(counted, 1)
                    if k or not first:
                        sum_groups(t - 1, (k - 1) % TC)

            tiles(0, True)
            with pe.Fori(1, T // TC) as it:
                tiles(it, False)
            sum_groups(T - 1, TC - 1)

        @block.vector
        def _(dve):
            dve.sem_inc(ring_used, GROUPS)
            dve.sem_inc(sums_used, 2)
            dve.sem_inc(cnt_used, 1)
            steps = Tally(dve, dve_step)
            nc.vector.memset(part[0:1, 0, :], -BIG).then_inc(low_ready, 1)
            steps.do(nc.vector.memset(ones[:, :], 1.0))
            steps.do(nc.vector.memset(need[:, :, :], 0.0))
            dve.wait_ge(x_in, 16)
            for k in range(3):
                nc.vector.tensor_copy(xs[:, k, :, :], nm[:, :, :]).then_inc(split, 1)
                dve.wait_ge(split, 2 * k + 1)
                if k < 2:
                    nc.vector.tensor_tensor(out=nm[:, :, :], in0=nm[:, :, :], in1=xs[:, k, :, :], op=ALU.subtract).then_inc(split, 1)
                    dve.wait_ge(split, 2 * k + 2)
            dve.wait_ge(low_in, 16)

            def single(t, e):
                hold(dve, sums_ready, t * (T // 8) + e + 1)
                nc.vector.tensor_reduce(part[:, GROUPS + e, :], sums[e % 2][:, :, :].rearrange("p g f -> p f g"), axis=AXX,
                                        op=ALU.max).then_inc(sums_used, 1)

            def extract(t, k, first=False):
                def bits(ap):
                    return ap.bitcast(I32)

                did = steps.did

                def do(ins, e=None):
                    did(ins)
                    if e is not None and not first:
                        single(t - 1, e)
                    steps.settle()

                c, x, y = counts[:, :], codes[:, :], many[:, :]
                hold(dve, counted, t + 1)
                do(nc.vector.tensor_copy(c, cnt[:, :]))
                nc.vector.tensor_scalar(pen[:, k % 2, :], c, 1.0, -BIG, ALU.not_equal, ALU.mult).then_inc(pen_ready, 1)
                did(nc.vector.tensor_reduce(deg[:, bass.ds(t, 1)], c, axis=AXX, op=ALU.add))
                do(nc.vector.tensor_scalar(several[:, :], c, 2.0, None, ALU.is_ge))
                did(nc.vector.tensor_tensor(out=x.rearrange("p (g w) -> p g w", w=WPG), in0=code_ps[:, :, :],
                                            in1=several[:, :].unsqueeze(2).to_broadcast([P, T, WPG]), op=ALU.mult))
                do(nc.vector.tensor_tensor(out=junk[:, :], in0=several[:, :], in1=c, op=ALU.mult), 0)
                dve.sem_inc(cnt_used, 1)
                did(nc.vector.tensor_reduce(due[:, bass.ds(t, 1)], junk[:, :], axis=AXX, op=ALU.add))
                do(nc.vector.tensor_scalar(bits(high[:, :]), bits(x), EXPONENT, None, ALU.bitwise_and))
                did(nc.vector.tensor_tensor(out=bits(keys[:, 0:NW]), in0=bits(high[:, :]), in1=code_no[:, :], op=ALU.bitwise_or))
                do(nc.vector.tensor_tensor(out=x, in0=x, in1=high[:, :], op=ALU.subtract), 1)
                do(nc.vector.tensor_tensor(out=bits(x), in0=bits(x), in1=code_no[:, :], op=ALU.bitwise_or))
                do(nc.vector.max(out=y, in_=x), 2)
                do(nc.vector.tensor_scalar(many_no[:, :], bits(y), NW - 1, None, ALU.bitwise_and))
                do(nc.vector.tensor_tensor(out=bits(y), in0=bits(y), in1=many_no[:, :], op=ALU.bitwise_xor))
                for d in range(DEEP - 1):
                    do(nc.vector.tensor_scalar(bits(many_high[:, :]), bits(y), EXPONENT, None, ALU.bitwise_and), 2 + d if d else None)
                    did(nc.vector.tensor_tensor(out=bits(keys[:, NW + d * MORE:NW + (d + 1) * MORE]), in0=bits(many_high[:, :]), in1=many_no[:, :], op=ALU.bitwise_or))
                    do(nc.vector.tensor_tensor(out=y, in0=y, in1=many_high[:, :], op=ALU.subtract))
                for r in range(SRT // 8):
                    do(nc.vector.max(out=srt[:, 8 * r:8 * r + 8], in_=keys[:, :]), 5 + r if r < 3 else None)
                    if r + 1 < SRT // 8:
                        do(nc.vector.match_replace(out=keys[:, :], in_to_replace=srt[:, 8 * r:8 * r + 8], in_values=keys[:, :], imm_value=0.0))
                did(nc.vector.tensor_scalar(bit[:, :], bits(srt[:, :]), 23, None, ALU.logical_shift_right))
                did(nc.vector.tensor_scalar(base[:, :], bits(srt[:, :]), NW - 1, 4, ALU.bitwise_and, ALU.logical_shift_left))
                do(nc.vector.tensor_scalar(pad[:, :], srt[:, :], 1.0, None, ALU.is_ge))
                did(nc.vector.tensor_reduce(found[:, bass.ds(t, 1)], pad[:, 0:SLOTS], axis=AXX, op=ALU.add))
                nc.vector.tensor_copy(need[:, k % 2, 0:GROUPS - SURE], pad[:, FIRST[SURE]:SLOTS:SIZES[-1]]).then_inc(need_made, 1)
                do(nc.vector.tensor_tensor(out=base[:, :], in0=base[:, :], in1=bit[:, :], op=ALU.add))
                do(nc.vector.scalar_tensor_tensor(out=pad[:, :], in0=base[:, :], scalar=-127.0 - N, in1=pad[:, :], op0=ALU.add, op1=ALU.mult))
                do(nc.vector.tensor_scalar(idx[:, k % 2, :], pad[:, :], float(N), None, ALU.add))
                dve.sem_inc(idx_ready, 1)

            def finish(t):
                for g in range(GROUPS):
                    if g < SURE:
                        hold(dve, gathered[g], (t + 1) * 16 * SIZES[g])
                    elif g == SURE:
                        hold(dve, rest_ready, t + 1)
                    nc.vector.tensor_reduce(part[:, g, :], ring[:, FIRST[g]:FIRST[g] + SIZES[g], :].rearrange("p k f -> p f k"), axis=AXX,
                                            op=ALU.max).then_inc(ring_used, 1)
                hold(dve, ring_used, (t + 2) * GROUPS)
                hold(dve, sums_used, (t + 1) * (T // 8) + 2)
                steps.do(nc.vector.tensor_reduce(nm[:, bass.ds(t, 1), :].rearrange("p o f -> p (o f)"), part[:, :, :].rearrange("p g f -> p f g"),
                                                 axis=AXX, op=ALU.max))

            extract(0, 0, True)
            with dve.Fori(0, T // 2 - 1) as it:
                for k in range(2):
                    extract(it * 2 + k + 1, k + 1)
                    finish(it * 2 + k)
            extract(T - 1, T - 1)
            finish(T - 2)
            for e in range(T // 8):
                single(T - 1, e)
            finish(T - 1)
            steps.do(nc.vector.tensor_tensor(out=due[:, :], in0=due[:, :], in1=found[:, :], op=ALU.not_equal))
            nc.vector.tensor_reduce(missed[:, :], due[:, :], axis=AXX, op=ALU.max).then_inc(missed_ready, 1)
            dve.wait_ge(missed_shared, 1)
            nc.vector.tensor_copy(flag[:, :], missed_all[:, :]).then_inc(flag_ready, 1)
            dve.wait_ge(flag_ready, 1)
            dve.wait_ge(stage_out, (NC + 1) * 16)
            more = dve.value_load(flag[0:1, 0:1], min_val=0, max_val=1)
            with dve.If(more != 0):
                dve.sem_inc(fb_adj_used, 1)
                dve.sem_inc(fb_step, 1)
                chunks = N // FJ
                with dve.Fori(0, T) as t:
                    hold(dve, fb_adj, (t + 1) * 16)
                    nc.vector.tensor_scalar(lim, adjb[:, :, :].rearrange("p h n -> p (h n)"), 0.0, 2.0, ALU.not_equal, ALU.mult).then_inc(nm_done, 1)
                    hold(dve, nm_done, t * 3 + 1)
                    nc.vector.tensor_scalar(lim, lim, -1.0, BIG, ALU.add, ALU.mult).then_inc(nm_done, 1)
                    nc.vector.memset(part[:, 0, :], -BIG).then_inc(nm_done, 1)
                    hold(dve, nm_done, t * 3 + 3)
                    with dve.Fori(0, chunks) as s:
                        n = (t * chunks + s) * 3 + 1
                        hold(dve, fb_x, (t * chunks + s + 1) * 16)
                        nc.vector.tensor_tensor(
                            out=tmp.rearrange("p (j f) -> p j f", f=F), in0=xb.rearrange("p (j f) -> p j f", f=F),
                            in1=lim[:, bass.ds(s * FJ, FJ)].unsqueeze(2).to_broadcast([P, FJ, F]), op=ALU.min).then_inc(fb_step, 1)
                        hold(dve, fb_step, n + 1)
                        nc.vector.tensor_reduce(part[:, 1, :], tmp.rearrange("p (j f) -> p f j", f=F), axis=AXX, op=ALU.max).then_inc(fb_step, 1)
                        hold(dve, fb_step, n + 2)
                        nc.vector.tensor_tensor(out=part[:, 0, :], in0=part[:, 0, :], in1=part[:, 1, :], op=ALU.max).then_inc(fb_step, 1)
                        hold(dve, fb_step, n + 3)
                    nc.vector.tensor_copy(nm[:, bass.ds(t, 1), :].rearrange("p o f -> p (o f)"), part[:, 0, :]).then_inc(fb_adj_used, 1)
                    hold(dve, fb_adj_used, t + 2)


def first_norm(nc, x, X, deg, has, stats):
    with ExitStack() as ctx:
        sem = SEMS[0]
        bn = ctx.enter_context(nc.sbuf_tensor("bn0", [P, T, 6], F32))
        xin = ctx.enter_context(nc.sbuf_tensor("xin", [P, T, F], F32))
        x_in, step, bn_done, ag_done = sem("x_again"), sem("step0"), sem("bn_done"), sem("ag_done")
        block = ctx.enter_context(nc.Block())

        @block.sync
        def _(sp):
            sp.dma_start(xin[:, :, :], x.rearrange("(t p) f -> p t f", p=P)).then_inc(x_in, 16)

        @block.vector
        def _(dve):
            s = Steps(dve, step)
            s.do(nc.vector.tensor_scalar(has[:, :], deg[:, :], 1.0, None, ALU.min))
            s.do(nc.vector.tensor_tensor(out=X[:, :, :], in0=X[:, :, :], in1=has[:, :].unsqueeze(2).to_broadcast([P, T, F]), op=ALU.mult))
            dve.wait_ge(x_in, 16)
            s.do(nc.vector.tensor_tensor(out=X[:, :, :], in0=X[:, :, :], in1=xin[:, :, :], op=ALU.add))
            for t in range(T):
                nc.vector.bn_stats(bn[:, t, :], X[:, t, :]).then_inc(bn_done, 1)
            dve.wait_ge(bn_done, T)
            for t in range(T):
                nc.vector.bn_aggr(stats[:, t, :], bn[:, t, :]).then_inc(ag_done, 1)
            dve.wait_ge(ag_done, T)


def normalise(nc, dve, act_sqrt, sqrt_done, s, X, stats, rstd):
    s.do(nc.vector.tensor_scalar(rstd[:, :], stats[:, :, 1], EPS, None, ALU.add))
    dve.sem_inc(act_sqrt, 1)
    s.do(nc.vector.tensor_tensor(out=X[:, :, :], in0=X[:, :, :], in1=stats[:, :, 0].unsqueeze(2).to_broadcast([P, T, F]), op=ALU.subtract))
    dve.wait_ge(sqrt_done, 1)
    s.do(nc.vector.reciprocal(rstd[:, :], rstd[:, :]))
    s.do(nc.vector.tensor_tensor(out=X[:, :, :], in0=X[:, :, :], in1=rstd[:, :].unsqueeze(2).to_broadcast([P, T, F]), op=ALU.mult))


def attention_layer(nc, layer, W, a_src, a_dst, mask_t, X, has, stats, rstd, ident, lastrow, nhd, dest):
    cut = layer == 1
    with ExitStack() as ctx:
        sb = lambda n, s, d: ctx.enter_context(nc.sbuf_tensor(f"{n}_{layer}", s, d))
        names = [0]

        def sem(n):
            names[0] += 1
            return SEMS[0](f"{n}_{layer}")

        XT = sb("XT", [P, N], F32)
        GX = sb("GX", [P, T, F], F32)
        Wn = sb("Wn", [P, F], F32)
        WT = sb("WT", [P, F], F32)
        Wa = None if cut else sb("Wa", [P, F + 1], F32)
        A3 = sb("A3", [P, 3], F32)
        U3 = sb("U3", [P, 3], F32)
        Urep = sb("Urep", [P, P], F32)
        sdh = sb("sdh", [P, T, 3], F32)
        dm = sb("dm", [P, 1], F32)
        D = sb("D", [P, 1], F32)
        nb = sb("nb", [P, 3], F32)
        E = sb("E", [P, T], F32)
        G = sb("G", [P, T], F32)
        zc = sb("zc", [P, 1], F32)
        mrow = sb("mrow", [1, F + 1], F32)
        cm = None if cut else sb("cm", [P, P], F32)
        bn = sb("bn", [P, TC, 6], F32)
        mv = sb("mv", [P, TC, 2], F32)
        banks = [ctx.enter_context(nc.psum_tensor(f"bank{i}_{layer}", [P, 512], F32)) for i in range(8)]

        with ExitStack() as pctx:
            psem = lambda n: SEMS[0](f"{n}_{layer}")
            if cut:
                B = pctx.enter_context(nc.sbuf_tensor("B_1", [P, T], F32))
                rest = pctx.enter_context(nc.sbuf_tensor("rest_1", [P, T], F32))
            w_in, act_sqrt, sqrt_done, step = psem("w_in"), psem("act_sqrt"), psem("sqrt_done"), psem("prep_step")
            x_ready, tr, ev = psem("x_ready"), psem("tr"), psem("ev")
            wt_ps, wt_sb, u_ps, u_sb = psem("wt_ps"), psem("wt_sb"), psem("u_ps"), psem("u_sb")
            cm_sb, wa_ps = psem("cm_sb"), psem("wa_ps")
            sd_ps, dm_sb, d_all, nb_sb, egb = psem("sd_ps"), psem("dm_sb"), psem("d_all"), psem("nb_sb"), psem("egb")
            mean_sb, mean_ps = psem("mean_sb"), psem("mean_ps")
            block = pctx.enter_context(nc.Block())
            NG = T // 4

            @block.sync
            def _(sp):
                sp.dma_start(Wn[:, :], W).then_inc(w_in, 16)
                sp.dma_start(A3[:, 0:1], a_src).then_inc(w_in, 16)
                sp.dma_start(A3[:, 1:2], a_dst).then_inc(w_in, 16)

            @block.gpsimd
            def _(pool):
                pool.wait_ge(dm_sb, 1)
                nc.gpsimd.partition_all_reduce(D[:, :], dm[:, :], P, bass.bass_isa.ReduceOp.max).then_inc(d_all, 1)

            @block.tensor
            def _(pe):
                pe.wait_ge(w_in, 48)
                nc.tensor.transpose(banks[4][:, 0:P], Wn[:, :], ident[:, :]).then_inc(wt_ps, 1)
                pe.wait_ge(wt_sb, 2)
                nc.tensor.matmul(banks[5][:, 0:3], WT[:, :], A3[:, :], start=True, stop=True).then_inc(u_ps, 1)
                if not cut:
                    pe.wait_ge(cm_sb, 1)
                    nc.tensor.matmul(banks[7][:, 0:F], cm[:, :], Wn[:, :], start=True, stop=True).then_inc(wa_ps, 1)
                pe.wait_ge(x_ready, 1)
                for g in range(NG):
                    if g >= 4:
                        pe.wait_ge(ev, g - 3)
                    for k in range(4):
                        last = nc.tensor.transpose(banks[g % 4][:, k * P:(k + 1) * P], X[:, 4 * g + k, :], ident[:, :])
                    last.then_inc(tr, 1)
                pe.wait_ge(u_sb, 2)
                pe.wait_ge(ev, NG)
                for t in range(T):
                    last = nc.tensor.matmul(banks[6][:, 3 * t:3 * t + 3], XT[:, t * P:(t + 1) * P], U3[:, :], start=True, stop=True)
                last.then_inc(sd_ps, 1)
                if not cut:
                    pe.wait_ge(mean_sb, 1)
                    nc.tensor.matmul(banks[4][0:1, 0:F], zc[:, :], Wn[:, :], start=True, stop=True).then_inc(mean_ps, 1)

            @block.scalar
            def _(act):
                act.wait_ge(act_sqrt, 1)
                nc.scalar.activation(rstd[:, :], rstd[:, :], ACT.Sqrt).then_inc(sqrt_done, 1)
                for g in range(NG):
                    act.wait_ge(tr, g + 1)
                    nc.scalar.activation(XT[:, g * CI:(g + 1) * CI], banks[g % 4][:, :], ACT.Copy).then_inc(ev, 1)
                act.wait_ge(nb_sb, 1)
                nc.scalar.activation(E[:, :], sdh[:, :, 1], ACT.Exp, bias=nb[:, 0:1], scale=0.8).then_inc(egb, 1)
                nc.scalar.activation(G[:, :], sdh[:, :, 1], ACT.Exp, bias=nb[:, 1:2], scale=0.2).then_inc(egb, 1)
                if cut:
                    nc.scalar.activation(B[:, :], sdh[:, :, 1], ACT.Exp, bias=nb[:, 2:3]).then_inc(egb, 1)

            @block.vector
            def _(dve):
                s = Steps(dve, step)
                if not cut:
                    s.do(nc.vector.tensor_tensor(out=cm[:, :], in0=ident[:, :], in1=lastrow[:, :], op=ALU.subtract))
                    dve.sem_inc(cm_sb, 1)
                normalise(nc, dve, act_sqrt, sqrt_done, s, X, stats, rstd)
                dve.sem_inc(x_ready, 1)
                nc.vector.memset(A3[:, 2:3], 1.0).then_inc(wt_sb, 1)
                dve.wait_ge(wt_ps, 1)
                nc.vector.tensor_copy(WT[:, :], banks[4][:, 0:P]).then_inc(wt_sb, 1)
                dve.wait_ge(u_ps, 1)
                nc.vector.tensor_copy(U3[:, :], banks[5][:, 0:3]).then_inc(u_sb, 1)
                dve.wait_ge(u_sb, 1)
                nc.vector.tensor_copy(Urep[:, :], U3[:, 0:1].to_broadcast([P, P])).then_inc(u_sb, 1)
                if not cut:
                    dve.wait_ge(wa_ps, 1)
                    s.do(nc.vector.tensor_copy(Wa[:, 0:F], banks[7][:, 0:F]))
                    s.do(nc.vector.tensor_copy(Wa[:, F:F + 1], lastrow[:, 0:1]))
                dve.wait_ge(sd_ps, 1)
                s.do(nc.vector.tensor_copy(sdh[:, :, :].rearrange("p t c -> p (t c)"), banks[6][:, 0:3 * T]))
                nc.vector.tensor_reduce(dm[:, :], sdh[:, :, 1], axis=AXX, op=ALU.max).then_inc(dm_sb, 1)
                dve.wait_ge(d_all, 1)
                for k, r in enumerate((-0.8, -0.2, -1.0)):
                    s.did(nc.vector.tensor_scalar(nb[:, k:k + 1], D[:, :], r, None, ALU.mult))
                s.settle()
                dve.sem_inc(nb_sb, 1)
                if not cut:
                    s.do(nc.vector.tensor_reduce(zc[:, :], XT[:, :], axis=AXX, op=ALU.add))
                    s.do(nc.vector.tensor_scalar(zc[:, :], zc[:, :], 1.0 / N, None, ALU.mult))
                    dve.sem_inc(mean_sb, 1)
                dve.wait_ge(egb, 3 if cut else 2)
                if cut:
                    v = sdh[:, :, 2]
                    s.do(nc.vector.tensor_scalar(v, v, 0.0, None, ALU.not_equal))
                    s.did(nc.vector.tensor_tensor(out=G[:, :], in0=G[:, :], in1=v, op=ALU.mult))
                    s.did(nc.vector.tensor_tensor(out=B[:, :], in0=B[:, :], in1=v, op=ALU.mult))
                    s.settle()
                s.did(nc.vector.tensor_tensor(out=GX[:, :, :], in0=X[:, :, :], in1=G[:, :].unsqueeze(2).to_broadcast([P, T, F]), op=ALU.mult))
                if cut:
                    s.do(nc.vector.memset(dest["tiny"][:, :], TINY))
                    s.do(nc.vector.memset(dest["kg"][:, :, :], 0.0))
                    s.do(nc.vector.memset(dest["km"][:, :, :], 0.0))
                    for src, at, out in ((B, 0, "km"), (G, 3, "km")):
                        s.do(nc.vector.tensor_scalar(rest[:, :], src[:, :], 0.5, None, ALU.mult))
                        for k in range(3):
                            part = dest[out][:, :, at + k]
                            s.do(nc.vector.tensor_copy(part, rest[:, :]))
                            s.do(nc.vector.tensor_tensor(out=rest[:, :], in0=rest[:, :], in1=part, op=ALU.subtract))
                    s.do(nc.vector.tensor_copy(dest["kg"][:, :, 0:3], dest["km"][:, :, 0:3]))
                    s.do(nc.vector.tensor_scalar(dest["kg"][:, :, 3:6], dest["km"][:, :, 3:6], -1.0, None, ALU.mult))
                    s.do(nc.vector.tensor_copy(dest["km"][:, :, 6], v))
                else:
                    s.settle()
                    s.do(nc.vector.tensor_copy(GX[:, :, F - 1], G[:, :]))
                    dve.wait_ge(mean_ps, 1)
                    s.did(nc.vector.tensor_copy(mrow[0:1, 0:F], banks[4][0:1, 0:F]))
                    s.did(nc.vector.memset(mrow[0:1, F:F + 1], 1.0))
                s.settle()

        m = sb("m", [P, 2, T, CI], FP8)
        w = sb("w", [P, WR, CI], F32)
        qb = sb("q", [P, 2, CI], F32)
        num = sb("num", [P, CI], F32)
        hp = sb("hp", [P, TC, F], F32)
        ex = num[:, :].rearrange("p (k f) -> p k f", f=F) if cut else sb("ex", [P, TC, F], F32)[:, :, :]
        rd = sb("rd", [P, TC], F32)
        z = sb("z", [P, 1 if cut else 2, CI], F32)
        nhc = None if cut else sb("nhc", [1, 2, CI], F32)
        z_ps, z_made, nh_in = sem("z_ps"), sem("z_made"), [sem("nh_in0"), sem("nh_in1")]
        if cut:
            signs = sb("signs", [P, AR, CI], BF16)
            u = sb("u", [P, 4, CI], BF16)
            den7 = sb("den7", [8, CI], F32)
            den = sb("den", [P, CI], F32)
            tiny = dest["tiny"]
            ratio = sb("ratio", [P, 2, CI], F32)
            theta = sb("theta", [P, 2, CI], F32)
        mask_in = [[sem(f"mask_in{b}{k}") for k in range(4)] for b in range(2)]
        q_ready, q_used, w_made, w_used = sem("q_ready"), sem("q_used"), sem("w_made"), sem("w_used")
        num_ready, num_used, acc_done = sem("num_ready"), sem("num_used"), sem("acc_done")
        post_ps, post_step, post_used, ex_done, mn_done = sem("post_ps"), sem("post_step"), sem("post_used"), sem("ex_done"), sem("mn_done")
        if cut:
            sign_made, low_done, den_made, g_made, g_used, u_made, den_ps, den_sb, rep_ps, chain, ln_done, th_done, rep_used = (
                sem(n) for n in ("sign_made", "low_done", "den_made", "g_made", "g_used", "u_made", "den_ps", "den_sb", "rep_ps", "chain", "ln_done", "th_done", "rep_used"))
        block = ctx.enter_context(nc.Block())
        acc = banks[0:2]
        hb = banks[2:4]
        PO = CI // 2
        made = [0]

        def chunks(eng, chunk, end, say_last=False):
            chunk(0, 0, True)
            with eng.Fori(0, NC // 2 - 1) as it:
                chunk(it * 2 + 1, 1, False)
                chunk(it * 2 + 2, 0, False)
            if say_last:
                chunk(NC - 1, 1, False, True)
            else:
                chunk(NC - 1, 1, False)
            end(NC - 1, 1)

        @block.sync
        def _(sp):
            def load(c, b, k):
                src = mask_t[bass.ds(c, 1), :, :].rearrange("c p (t n) -> p (c t) n", n=CI)
                sp.dma_start(m[:, b, k * QJ:(k + 1) * QJ, :].bitcast(U8), src[:, k * QJ:(k + 1) * QJ, :]).then_inc(mask_in[b][k], 16)

            for b in range(2):
                for k in range(4):
                    load(b, b, k)
            with sp.Fori(0, NC // 2 - 1) as it:
                for b in range(2):
                    for k in range(4):
                        hold(sp, w_made, (it * 2 + b) * T + (k + 1) * QJ)
                        load(it * 2 + b + 2, b, k)

        if cut:
            @block.gpsimd
            def _(pool):
                signs_in, chain_steps = Tally(pool, sign_made), Tally(pool, chain)

                def chunk(c, b):
                    for j in range(T):
                        if j % QJ == 0:
                            hold(pool, mask_in[b][j // QJ], (c - b + 2) * 8)
                        signs_in.wait()
                        nc.gpsimd.tensor_tensor(out=signs[:, j % AR, :], in0=signs[:, j % AR, :], in1=m[:, b, j, :], op=ALU.mult).then_inc(g_made, 1)
                    s = chain_steps
                    hold(pool, ln_done, c + 1)
                    s.do(nc.gpsimd.tensor_tensor(out=z[:, 0, :], in0=z[:, 0, :], in1=theta[:, b, :], op=ALU.add))
                    hold(pool, low_done, c + 1)
                    s.do(nc.gpsimd.tensor_tensor(out=theta[:, b, :], in0=theta[:, b, :], in1=z[:, 0, :], op=ALU.subtract))

                with pool.Fori(0, NC // 2) as it:
                    chunk(it * 2, 0)
                    chunk(it * 2 + 1, 1)

        else:
            @block.gpsimd
            def _(pool):
                def load(c, b):
                    pool.dma_start(nhc[0:1, b, :], nhd[:, bass.ds(c * CI, CI)]).then_inc(nh_in[b], 16)

                for b in range(2):
                    load(b, b)
                with pool.Fori(0, NC // 2 - 1) as it:
                    for b in range(2):
                        hold(pool, post_ps, it * 2 + b + 1)
                        load(it * 2 + b + 2, b)

        @block.tensor
        def _(pe):
            def row_terms(c):
                if cut:
                    pe.wait_ge(rep_used, c + 1)
                nc.tensor.matmul(banks[7][:, :], Urep[:, :], XT[:, bass.ds(c * CI, CI)], start=True, stop=True).then_inc(z_ps, 1)

            def post(c, b):
                if not cut:
                    pe.wait_ge(nh_in[b], (c - b + 2) * 8)
                pe.wait_ge(num_ready, c + 1)
                pe.wait_ge(post_used, c + 1)
                for k in range(TC):
                    out = hb[k // 2]
                    o = (k % 2) * PO
                    lhs = num[:, k * P:(k + 1) * P]
                    if cut:
                        last = nc.tensor.matmul(out[:, o:o + F], lhs, Wn[:, :], start=True, stop=True)
                    else:
                        nc.tensor.matmul(out[:, o:o + F + 1], lhs, Wa[:, :], start=True, stop=False)
                        last = nc.tensor.matmul(out[:, o:o + F + 1], nhc[0:1, b, k * P:(k + 1) * P], mrow[0:1, :], start=False, stop=True)
                last.then_inc(post_ps, 1)

            def denominator(c, b, j):
                g_in_order.wait()
                nc.tensor.matmul(banks[4][0:8, :], dest["kg"][:, j, :], signs[:, j % AR, :], start=(j == 0), stop=False)
                nc.tensor.matmul(banks[4][0:8, :], dest["km"][:, j, :], m[:, b, j, :], start=False, stop=(j == T - 1)).then_inc(g_used, 1)

            def spread(c):
                pe.wait_ge(den_sb, c + 1)
                pe.wait_ge(z_made, c + 1)
                for k in range(3):
                    last = nc.tensor.matmul(banks[5 + k][:, :], dest["sel"][0:8, k, :], den7[:, :], start=True, stop=True)
                last.then_inc(rep_ps, 1)

            def chunk(c, b, first, last_chunk=False):
                if first:
                    row_terms(0)
                    if cut:
                        for j in range(T):
                            denominator(0, 0, j)
                        spread(0)
                if cut and not last_chunk:
                    row_terms(c + 1)
                ahead = 0
                for j in range(T):
                    if j == (24 if cut else 8) and not first:
                        post(c - 1, 1 - b)
                    if j == 32 and not last_chunk and not cut:
                        row_terms(c + 1)
                    if cut and not last_chunk:
                        while ahead < min(T, (j - 2) * 4 // 3):
                            denominator(c + 1, 1 - b, ahead)
                            ahead += 1
                        if j == SPREAD_AT:
                            spread(c + 1)
                    w_in_order.wait()
                    last = nc.tensor.matmul(acc[b][:, :], GX[:, j, :], w[:, j % WR, :], start=(j == 0), stop=(j == T - 1))
                    last.then_inc(w_used, 1)

            w_in_order = Tally(pe, w_made)
            g_in_order = Tally(pe, g_made) if cut else None
            chunks(pe, chunk, post, True)

        @block.scalar
        def _(act):
            def take(c, b):
                hold(act, w_used, WR + (c + 1) * T)
                hold(act, num_used, c + 1)
                if not cut:
                    nc.scalar.activation(num[:, :], acc[b][:, :], ACT.Copy).then_inc(num_ready, 1)

            def expo(c):
                hold(act, mn_done, c + 1)
                nc.scalar.activation(ex, ex, ACT.Exp).then_inc(ex_done, 1)

            def chunk(c, b, first):
                hold(act, q_used, c + 1)
                hold(act, z_ps, c + 1)
                nc.scalar.activation(z[:, b, :], banks[7][:, :], ACT.Relu, bias=D[:, 0:1]).then_inc(z_made, 1)
                hold(act, z_made, c + 1)
                nc.scalar.activation(qb[:, b, :], z[:, b, :], ACT.Exp, scale=-0.8).then_inc(q_ready, 1)
                if not first:
                    take(c - 1, 1 - b)
                    expo(c - 1)

            def row_values(c, b):
                hold(act, q_used, c + 1)
                hold(act, z_ps, c + 1)
                nc.scalar.activation(z[:, 0, :], banks[7][:, :], ACT.Relu, bias=D[:, 0:1]).then_inc(z_made, 1)
                hold(act, z_made, c + 1)
                nc.scalar.activation(qb[:, b, :], z[:, 0, :], ACT.Exp, scale=-0.8).then_inc(q_ready, 1)

            def signs_and_limits(c, b, expo_of=None):
                for j in range(T):
                    if j == EXPO_AT and expo_of is not None:
                        expo(expo_of)
                    signs_free.wait()
                    nc.scalar.activation(signs[:, j % AR, :], qb[:, b, :], ACT.Sign, bias=E[:, j:j + 1], scale=-1.0).then_inc(sign_made, 1)
                hold(act, g_used, AR + (c + 1) * T)
                nc.scalar.activation(den7[:, :], banks[4][0:8, :], ACT.Copy).then_inc(den_sb, 1)
                hold(act, den_made, c + 1)
                nc.scalar.activation(theta[:, b, :], den[:, :], ACT.Ln, scale=THR, bias=tiny[:, 0:1]).then_inc(ln_done, 1)
                hold(act, chain, c * CHAIN + 1)
                nc.scalar.activation(z[:, 0, :], z[:, 0, :], ACT.Relu, scale=-4.0).then_inc(low_done, 1)
                hold(act, chain, c * CHAIN + 2)
                nc.scalar.activation(theta[:, b, :], theta[:, b, :], ACT.Exp, scale=0.8).then_inc(th_done, 1)

            def cut_chunk(c, b, first):
                if first:
                    row_values(0, 0)
                    hold(act, q_ready, 1)
                    signs_and_limits(0, 0)
                row_values(c + 1, 1 - b)
                hold(act, q_ready, c + 2)
                signs_and_limits(c + 1, 1 - b, None if first else c - 1)

            signs_free = Tally(act, g_used) if cut else None
            if cut:
                act.sem_inc(g_used, AR)

            def end(c, b):
                take(c, b)
                expo(c)

            if cut:
                cut_chunk(0, 0, True)
                with act.Fori(0, NC // 2 - 1) as it:
                    cut_chunk(it * 2 + 1, 1, False)
                    cut_chunk(it * 2 + 2, 0, False)
                expo(NC - 2)
                expo(NC - 1)
            else:
                chunks(act, chunk, end)

        @block.vector
        def _(dve):
            dve.sem_inc(post_used, 1)
            dve.sem_inc(num_used, 1)
            dve.sem_inc(w_used, WR)
            if cut:
                dve.sem_inc(rep_used, 1)
            dve.sem_inc(q_used, 2)
            w_free = Tally(dve, w_used)
            post_steps = Tally(dve, post_step)
            if cut:
                u_done = Tally(dve, u_made)

            def scale_sums(c, b):
                hold(dve, w_used, WR + (c + 1) * T)
                s = post_steps
                s.do(nc.vector.tensor_tensor(out=num[:, :], in0=acc[b][:, :], in1=ratio[:, b, :], op=ALU.mult))
                s.did(nc.vector.tensor_tensor(out=num[:, :], in0=num[:, :], in1=XT[:, bass.ds(c * CI, CI)], op=ALU.add))
                s.settle()
                dve.sem_inc(num_ready, 1)

            def ratios(c, b, ln=True):
                hold(dve, rep_ps, c + 1)
                if ln:
                    hold(dve, ln_done, c)
                post_steps.do(nc.vector.tensor_tensor(out=den[:, :], in0=banks[6][:, :], in1=qb[:, b, :], op=ALU.mult))
                post_steps.do(nc.vector.tensor_tensor(out=den[:, :], in0=den[:, :], in1=banks[5][:, :], op=ALU.add))
                dve.sem_inc(den_made, 1)
                post_steps.do(nc.vector.tensor_scalar(ratio[:, b, :], den[:, :], TINY, None, ALU.max))
                post_steps.do(nc.vector.reciprocal(ratio[:, b, :], ratio[:, b, :]))
                post_steps.do(nc.vector.tensor_tensor(out=ratio[:, b, :], in0=banks[7][:, :], in1=ratio[:, b, :], op=ALU.mult))
                dve.sem_inc(rep_used, 1)

            def post(c, b):
                hold(dve, post_ps, c + 1)
                dve.sem_inc(num_used, 1)
                s = post_steps
                raw = [hb[k // 2][:, (k % 2) * PO:(k % 2) * PO + F + 1] for k in range(TC)]
                if cut:
                    for k in range(2):
                        s.did(nc.vector.tensor_copy(hp[:, 2 * k:2 * k + 2, :], hb[k][:, :].rearrange("p (a n) -> p a n", a=2)[:, :, 0:F]))
                    s.settle()
                else:
                    for k in range(2):
                        s.did(nc.vector.reciprocal(rd[:, 2 * k:2 * k + 2], hb[k][:, :].rearrange("p (a n) -> p a n", a=2)[:, :, F]))
                    s.settle()
                    for k in range(2):
                        s.did(nc.vector.tensor_tensor(out=hp[:, 2 * k:2 * k + 2, :], in0=hb[k][:, :].rearrange("p (a n) -> p a n", a=2)[:, :, 0:F],
                                                      in1=rd[:, 2 * k:2 * k + 2].unsqueeze(2).to_broadcast([P, 2, F]), op=ALU.mult))
                    s.settle()
                dve.sem_inc(post_used, 1)
                nc.vector.tensor_scalar(ex, hp[:, :, :], 0.0, None, ALU.min).then_inc(mn_done, 1)

            def post_rest(c, b):
                s = post_steps
                hold(dve, ex_done, c + 1)
                s.do(nc.vector.scalar_tensor_tensor(out=hp[:, :, :], in0=hp[:, :, :], scalar=0.0, in1=ex, op0=ALU.max, op1=ALU.add))
                xc = X[:, bass.ds(c * TC, TC), :]
                s.do(nc.vector.scalar_tensor_tensor(out=xc, in0=hp[:, :, :], scalar=-1.0, in1=xc, op0=ALU.add, op1=ALU.add))
                for k in range(TC):
                    last = nc.vector.bn_stats(bn[:, k, :], X[:, bass.ds(c * TC + k, 1), :].rearrange("p o f -> p (o f)"))
                s.do(last)
                for k in range(TC):
                    last = nc.vector.bn_aggr(mv[:, k, :], bn[:, k, :])
                s.do(last)
                s.do(nc.vector.tensor_copy(stats[:, bass.ds(c * TC, TC), :], mv[:, :, :]))

            def chunk(c, b, first, last_chunk=False):
                q = qb[:, b, :]
                hold(dve, q_ready, c + 1)
                if cut:
                    if first:
                        ratios(0, 0, False)
                    hold(dve, th_done, c + 1)

                    def keep(j):
                        if j % QJ == 0:
                            hold(dve, mask_in[b][j // QJ], wait_of(c, b))
                        nc.vector.scalar_tensor_tensor(out=u[:, j % 4, :], in0=theta[:, b, :], scalar=E[:, j:j + 1], in1=m[:, b, j, :],
                                                       op0=ALU.is_le, op1=ALU.mult).then_inc(u_made, 1)

                    keep(0)
                    for j in range(T):
                        if j + 1 < T:
                            keep(j + 1)
                        u_done.wait()
                        w_free.wait()
                        nc.vector.scalar_tensor_tensor(out=w[:, j % WR, :], in0=q, scalar=E[:, j:j + 1], in1=u[:, j % 4, :],
                                                       op0=ALU.max, op1=ALU.mult).then_inc(w_made, 1)
                        if j == 16 and not first:
                            scale_sums(c - 1, 1 - b)
                        if j == 28 and not first:
                            post(c - 1, 1 - b)
                        if j == 42 and not first:
                            post_rest(c - 1, 1 - b)
                        if j == RATIOS_AT and not last_chunk:
                            ratios(c + 1, 1 - b)
                else:
                    for j in range(T):
                        if j % QJ == 0:
                            hold(dve, mask_in[b][j // QJ], wait_of(c, b))
                        w_free.wait()
                        nc.vector.scalar_tensor_tensor(out=w[:, j % WR, :], in0=q, scalar=E[:, j:j + 1], in1=m[:, b, j, :],
                                                       op0=ALU.max, op1=ALU.mult).then_inc(w_made, 1)
                        if j == 24 and not first:
                            post(c - 1, 1 - b)
                        if j == 28 and not first:
                            post_rest(c - 1, 1 - b)
                hold(dve, w_made, (c + 1) * T)
                dve.sem_inc(q_used, 1)

            def wait_of(c, b):
                return (c - b + 2) * 8

            def end(c, b):
                if cut:
                    scale_sums(c, b)
                post(c, b)
                post_rest(c, b)

            chunks(dve, chunk, end, True)


def program(nc, x, adj, W1, a1, W2, a2, W3, a3, out):
    mask_t = nc.dram_tensor("mask_t", [NC, P, T * CI], U8, kind="Internal").ap()
    x_ext = nc.dram_tensor("x_ext", [N + 1, F], F32, kind="Internal").ap()
    nhd = nc.dram_tensor("nhd", [1, N], F32, kind="Internal").ap()
    with ExitStack() as ctx:
        SPARE[:] = [ctx.enter_context(nc.semaphore("spare"))]
        sb = lambda n, s, d: ctx.enter_context(nc.sbuf_tensor(n, s, d))
        X = sb("X", [P, T, F], F32)
        ident = sb("ident", [P, P], F32)
        lastrow = sb("lastrow", [P, P], F32)
        deg = sb("deg", [P, T], F32)
        has = sb("has", [P, T], F32)
        stats = sb("stats", [P, T, 2], F32)
        rstd = sb("rstd", [P, T], F32)
        sel = sb("sel", [8, 3, P], F32)

        with Phase(nc), ExitStack() as c0:
            sb0 = lambda n, s, d: c0.enter_context(nc.sbuf_tensor(n, s, d))
            ident_b = sb0("ident_b", [P, P], BF16)
            powers = sb0("powers", [P, WPG], BF16)
            code_no = sb0("code_no", [P, NW], I32)
            with ExitStack() as c1:
                power_i = c1.enter_context(nc.sbuf_tensor("power_i", [P, WPG], I32))
                made, used, again = (SEMS[0](n) for n in ("made", "used", "again"))
                block = c1.enter_context(nc.Block())

                @block.gpsimd
                def _(pool):
                    s = Steps(pool, made)
                    s.do(nc.gpsimd.memset(ident[:, :], 0.0))
                    s.do(nc.gpsimd.affine_select(out=ident[:, :], in_=ident[:, :], compare_op=ALU.not_equal, fill=1.0, base=0, pattern=[[-1, P]], channel_multiplier=1))
                    s.do(nc.gpsimd.memset(lastrow[:, :], 0.0))
                    s.do(nc.gpsimd.affine_select(out=lastrow[:, :], in_=lastrow[:, :], compare_op=ALU.not_equal, fill=1.0, base=-(P - 1), pattern=[[0, P]], channel_multiplier=1))
                    s.do(nc.gpsimd.iota(power_i[:, :], pattern=[[-WORD, WPG]], base=127, channel_multiplier=1))
                    pool.wait_ge(used, 2)
                    power_f = power_i[:, :].bitcast(F32)
                    s.do(nc.gpsimd.affine_select(out=power_f, in_=power_f, compare_op=ALU.is_ge, fill=0.0, base=0, pattern=[[-WORD, WPG]], channel_multiplier=1))
                    s.do(nc.gpsimd.affine_select(out=power_f, in_=power_f, compare_op=ALU.is_ge, fill=0.0, base=WORD - 1, pattern=[[WORD, WPG]], channel_multiplier=-1))
                    s.do(nc.gpsimd.iota(code_no[:, :], pattern=[[1, NW]], base=0, channel_multiplier=0))
                    s.do(nc.gpsimd.memset(sel[:, :, :], 1.0))
                    for k in range(3):
                        s.do(nc.gpsimd.affine_select(out=sel[:, k, :], in_=sel[:, k, :], compare_op=ALU.is_ge, fill=0.0, base=-3 * k, pattern=[[0, P]], channel_multiplier=1))
                        hi = (2, 5, 6)[k]
                        s.do(nc.gpsimd.affine_select(out=sel[:, k, :], in_=sel[:, k, :], compare_op=ALU.is_ge, fill=0.0, base=hi, pattern=[[0, P]], channel_multiplier=-1))

                @block.vector
                def _(dve):
                    dve.wait_ge(made, 5)
                    nc.vector.tensor_copy(ident_b[:, :], ident[:, :]).then_inc(used, 1)
                    nc.vector.tensor_scalar(power_i[:, :], power_i[:, :], 23, None, ALU.logical_shift_left).then_inc(used, 1)
                    dve.wait_ge(made, 7)
                    nc.vector.tensor_copy(powers[:, :], power_i[:, :].bitcast(F32)).then_inc(again, 1)
                    dve.wait_ge(again, 1)

            neighbour_max(nc, x, adj, mask_t, x_ext, X, deg, (ident_b, powers, code_no))
            first_norm(nc, x, X, deg, has, stats)

        with Phase(nc), ExitStack() as c2:
            nohas = c2.enter_context(nc.sbuf_tensor("nohas", [P, T], F32))
            nhT = c2.enter_context(nc.sbuf_tensor("nhT", [T, P], F32))
            tps = c2.enter_context(nc.psum_tensor("tps", [T, P], F32))
            a, b, c, d = (SEMS[0](n) for n in ("nh_a", "nh_b", "nh_c", "nh_d"))
            block = c2.enter_context(nc.Block())

            @block.vector
            def _(dve):
                nc.vector.tensor_scalar(nohas[:, :], has[:, :], -1.0, 1.0, ALU.mult, ALU.add).then_inc(a, 1)
                dve.wait_ge(b, 1)
                nc.vector.tensor_copy(nhT[:, :], tps[:, :]).then_inc(c, 1)

            @block.tensor
            def _(pe):
                pe.wait_ge(a, 1)
                nc.tensor.transpose(tps[:, :], nohas[:, :], ident[:, :]).then_inc(b, 1)

            @block.sync
            def _(sp):
                sp.wait_ge(c, 1)
                sp.dma_start(nhd.rearrange("o (t p) -> (o t) p", p=P), nhT[:, :]).then_inc(d, 16)
                sp.wait_ge(d, 16)

        kg = sb("kg", [P, T, 8], BF16)
        km = sb("km", [P, T, 8], BF16)
        tiny = sb("tiny", [P, 1], F32)
        dest = {"kg": kg, "km": km, "sel": sel, "tiny": tiny}
        with Phase(nc):
            attention_layer(nc, 1, W1, a1[0:F, :], a1[F:2 * F, :], mask_t, X, has, stats, rstd, ident, lastrow, nhd, dest)
        with Phase(nc):
            attention_layer(nc, 2, W2, a2[0:F, :], a2[F:2 * F, :], mask_t, X, has, stats, rstd, ident, lastrow, nhd, dest)
        with Phase(nc):
            attention_layer(nc, 3, W3, a3[F:2 * F, :], a3[0:F, :], mask_t, X, has, stats, rstd, ident, lastrow, nhd, dest)

        with Phase(nc), ExitStack() as c3:
            step, want, got, done, ready = (SEMS[0](n) for n in ("fstep", "want", "got", "written", "ready"))
            block = c3.enter_context(nc.Block())

            @block.vector
            def _(dve):
                normalise(nc, dve, want, got, Steps(dve, step), X, stats, rstd)
                dve.sem_inc(ready, 1)

            @block.scalar
            def _(act):
                act.wait_ge(want, 1)
                nc.scalar.activation(rstd[:, :], rstd[:, :], ACT.Sqrt).then_inc(got, 1)

            @block.sync
            def _(sp):
                sp.wait_ge(ready, 1)
                sp.dma_start(out.rearrange("(t p) f -> p t f", p=P), X[:, :, :]).then_inc(done, 16)
                sp.wait_ge(done, 16)


_INS = ["x", "adj", "L1_gnn_W", "L1_gnn_a", "L2_gnn_W", "L2_gnn_a", "L3_gnn_W", "L3_gnn_a"]


def kernel(**inputs):
    import numpy as np
    import concourse.bacc as bacc
    from concourse.bass_utils import run_bass_kernel_spmd

    nc = bacc.Bacc("TRN2", target_bir_lowering=False, num_devices=1)
    arrays, args = {}, []
    for name in _INS:
        a = np.ascontiguousarray(inputs[name])
        if a.ndim == 1:
            a = a.reshape(-1, 1)
        arrays[f"in_{name}"] = a
        args.append(nc.dram_tensor(f"in_{name}", a.shape, mybir.dt.from_np(a.dtype), kind="ExternalInput").ap())
    out = nc.dram_tensor("out", (N, F), F32, kind="ExternalOutput").ap()
    program(nc, *args, out)
    r = run_bass_kernel_spmd(nc, [arrays], core_ids=[0])
    return r.results[0]["out"]
```
